# Optimizing a Trainium2 kernel written in Bass

```python
import numpy as np
import jax
import jax.numpy as jnp

def _softmax(x, axis=-1):
    return jax.nn.softmax(x, axis=axis)

def _gelu(x):
    return jax.nn.gelu(x, approximate=True)

def _silu(x):
    return jax.nn.silu(x)

def _sigmoid(x):
    return jax.nn.sigmoid(x)

def _layernorm(x, axis=-1, eps=1e-05):
    m = jnp.mean(x, axis=axis, keepdims=True)
    v = jnp.var(x, axis=axis, keepdims=True)
    return (x - m) / jnp.sqrt(v + eps)

def _scatter_add(tgt, idx, src, axis=0):
    return tgt.at[idx].add(src)

def _segment_sum(src, seg, n):
    return jax.ops.segment_sum(src, seg, n)
kernel_name = 'mk_cond_seq_d2_seqx_r4_deab61'

def setup_inputs(seed: int=0):
    np.random.seed(seed)
    _w = jnp.asarray

    def _rec_inputs():
        import jax
        import jax.numpy as jnp
        _rk = jax.random.key(seed)
        x = -0.0003482 + 1 * jax.random.normal(jax.random.fold_in(_rk, 1), (128, 64, 288), jnp.float32)
        _lenS = 64 - jax.random.randint(jax.random.fold_in(_rk, 7), (128,), 0, max(1, 64 // 4) + 1, jnp.int32)
        _lenS2 = 64 - jax.random.randint(jax.random.fold_in(_rk, 8), (128,), 0, max(1, 64 // 4) + 1, jnp.int32)
        cond_1152 = 0.00257642 + 1.0011 * jax.random.normal(jax.random.fold_in(_rk, 11), (128, 288), jnp.float32)
        return (x, cond_1152)
    x, cond_1152 = _rec_inputs()

    def _L0_cond_setup():
        import jax, jax.numpy as jnp
        import numpy as np
        H = 288
        NH = 16
        HD = H // NH
        MLP = int(H * 4.0)
        EPS = 1e-06

        def _ln(z, scale=None):
            m = jnp.mean(z, axis=-1, keepdims=True)
            v = jnp.mean(jnp.square(z - m), axis=-1, keepdims=True)
            y = (z - m) * jax.lax.rsqrt(v + EPS)
            if scale is not None:
                y = y * scale
            return y
        key = jax.random.key(seed)
        ks = jax.random.split(key, 16)
        B, N = (16, 256)
        x = jax.random.normal(ks[0], (B, N, H), dtype=jnp.float32)
        c = jax.random.normal(ks[1], (B, H), dtype=jnp.float32)

        def xav(k, fan_in, fan_out):
            lim = np.sqrt(6.0 / (fan_in + fan_out))
            return jax.random.uniform(k, (fan_in, fan_out), jnp.float32, -lim, lim)
        w_mod = 0.02 * jax.random.normal(ks[2], (H, 6 * H), dtype=jnp.float32)
        b_mod = 0.02 * jax.random.normal(ks[3], (6 * H,), dtype=jnp.float32)
        w_qkv = xav(ks[4], H, 3 * H)
        b_qkv = jnp.zeros((3 * H,), jnp.float32)
        g_q = jnp.ones((HD,), jnp.float32)
        g_k = jnp.ones((HD,), jnp.float32)
        w_proj = xav(ks[5], H, H)
        b_proj = jnp.zeros((H,), jnp.float32)
        w1 = xav(ks[6], H, MLP)
        b1 = jnp.zeros((MLP,), jnp.float32)
        w2 = xav(ks[7], MLP, H)
        b2 = jnp.zeros((H,), jnp.float32)
        return dict(x=x, c=c, w_mod=w_mod, b_mod=b_mod, w_qkv=w_qkv, b_qkv=b_qkv, g_q=g_q, g_k=g_k, w_proj=w_proj, b_proj=b_proj, w1=w1, b1=b1, w2=w2, b2=b2)
    _L0_cond_all = _L0_cond_setup()
    _L0_cond_in = {k: v for k, v in _L0_cond_all.items() if k in ('w_mod', 'b_mod', 'w_qkv', 'b_qkv', 'g_q', 'g_k', 'w_proj', 'b_proj', 'w1', 'b1', 'w2', 'b2')}
    del _L0_cond_all

    def _L1_cond_setup():
        import jax, jax.numpy as jnp
        import numpy as np
        B, L, C = (8, 256, 288)
        H = 16
        D = C // H
        FF = int(C * 4.0)
        EPS = 1e-06

        def _layernorm(x):
            mu = jnp.mean(x, axis=-1, keepdims=True)
            var = jnp.mean(jnp.square(x - mu), axis=-1, keepdims=True)
            return (x - mu) * jax.lax.rsqrt(var + EPS)

        def _modulate(x, shift, scale):
            return x * (1.0 + scale) + shift

        def _attention(h, W_qkv, b_qkv, W_proj, b_proj):
            b, l, c = h.shape
            qkv = h @ W_qkv + b_qkv
            qkv = qkv.reshape(b, l, 3, H, D)
            q, k, v = (qkv[:, :, 0], qkv[:, :, 1], qkv[:, :, 2])
            scale = D ** (-0.5)
            scores = jnp.einsum('blhd,bmhd->bhlm', q * scale, k)
            attn = jax.nn.softmax(scores, axis=-1)
            o = jnp.einsum('bhlm,bmhd->blhd', attn, v).reshape(b, l, c)
            return o @ W_proj + b_proj
        key = jax.random.key(seed)
        ks = jax.random.split(key, 12)
        s = 0.02
        return {'x': jax.random.normal(ks[0], (B, L, C), jnp.float32), 'c': jax.random.normal(ks[1], (B, 1, C), jnp.float32), 'W_qkv': jax.random.normal(ks[2], (C, 3 * C), jnp.float32) * s, 'b_qkv': jnp.zeros((3 * C,), jnp.float32), 'W_proj': jax.random.normal(ks[3], (C, C), jnp.float32) * s, 'b_proj': jnp.zeros((C,), jnp.float32), 'W_fc1': jax.random.normal(ks[4], (C, FF), jnp.float32) * s, 'b_fc1': jnp.zeros((FF,), jnp.float32), 'W_fc2': jax.random.normal(ks[5], (FF, C), jnp.float32) * s, 'b_fc2': jnp.zeros((C,), jnp.float32), 'W_ada': jax.random.normal(ks[6], (C, 6 * C), jnp.float32) * s, 'b_ada': jnp.zeros((6 * C,), jnp.float32)}
    _L1_cond_all = _L1_cond_setup()
    _L1_cond_in = {k: v for k, v in _L1_cond_all.items() if k in ('W_qkv', 'b_qkv', 'W_proj', 'b_proj', 'W_fc1', 'b_fc1', 'W_fc2', 'b_fc2', 'W_ada', 'b_ada')}
    del _L1_cond_all
    return {'x': x, 'cond_1152': cond_1152, 'L0_cond_w_mod': _L0_cond_in['w_mod'], 'L0_cond_b_mod': _L0_cond_in['b_mod'], 'L0_cond_w_qkv': _L0_cond_in['w_qkv'], 'L0_cond_b_qkv': _L0_cond_in['b_qkv'], 'L0_cond_g_q': _L0_cond_in['g_q'], 'L0_cond_g_k': _L0_cond_in['g_k'], 'L0_cond_w_proj': _L0_cond_in['w_proj'], 'L0_cond_b_proj': _L0_cond_in['b_proj'], 'L0_cond_w1': _L0_cond_in['w1'], 'L0_cond_b1': _L0_cond_in['b1'], 'L0_cond_w2': _L0_cond_in['w2'], 'L0_cond_b2': _L0_cond_in['b2'], 'L1_cond_W_qkv': _L1_cond_in['W_qkv'], 'L1_cond_b_qkv': _L1_cond_in['b_qkv'], 'L1_cond_W_proj': _L1_cond_in['W_proj'], 'L1_cond_b_proj': _L1_cond_in['b_proj'], 'L1_cond_W_fc1': _L1_cond_in['W_fc1'], 'L1_cond_b_fc1': _L1_cond_in['b_fc1'], 'L1_cond_W_fc2': _L1_cond_in['W_fc2'], 'L1_cond_b_fc2': _L1_cond_in['b_fc2'], 'L1_cond_W_ada': _L1_cond_in['W_ada'], 'L1_cond_b_ada': _L1_cond_in['b_ada']}

def reference(x, cond_1152, L0_cond_w_mod, L0_cond_b_mod, L0_cond_w_qkv, L0_cond_b_qkv, L0_cond_g_q, L0_cond_g_k, L0_cond_w_proj, L0_cond_b_proj, L0_cond_w1, L0_cond_b1, L0_cond_w2, L0_cond_b2, L1_cond_W_qkv, L1_cond_b_qkv, L1_cond_W_proj, L1_cond_b_proj, L1_cond_W_fc1, L1_cond_b_fc1, L1_cond_W_fc2, L1_cond_b_fc2, L1_cond_W_ada, L1_cond_b_ada):
    import jax
    import jax.numpy as jnp

    def _L0_cond_ref(x, c, w_mod, b_mod, w_qkv, b_qkv, g_q, g_k, w_proj, b_proj, w1, b1, w2, b2):
        import jax, jax.numpy as jnp
        import numpy as np
        H = 288
        NH = 16
        HD = H // NH
        MLP = int(H * 4.0)
        EPS = 1e-06

        def _ln(z, scale=None):
            m = jnp.mean(z, axis=-1, keepdims=True)
            v = jnp.mean(jnp.square(z - m), axis=-1, keepdims=True)
            y = (z - m) * jax.lax.rsqrt(v + EPS)
            if scale is not None:
                y = y * scale
            return y
        B, N, _ = x.shape
        mod = jax.nn.swish(c) @ w_mod + b_mod
        sh_msa, sc_msa, g_msa, sh_mlp, sc_mlp, g_mlp = jnp.split(mod, 6, axis=1)
        xn = _ln(x) * (1 + sc_msa[:, None, :]) + sh_msa[:, None, :]
        qkv = xn @ w_qkv + b_qkv
        qkv = qkv.reshape(B, N, 3, NH, HD).transpose(2, 0, 3, 1, 4)
        q, k, v = (qkv[0], qkv[1], qkv[2])
        q = _ln(q, g_q)
        k = _ln(k, g_k)
        attn = jax.nn.softmax(jnp.einsum('bhqd,bhkd->bhqk', q, k) * HD ** (-0.5), axis=-1)
        o = jnp.einsum('bhqk,bhkd->bhqd', attn, v)
        o = o.transpose(0, 2, 1, 3).reshape(B, N, H) @ w_proj + b_proj
        x = x + g_msa[:, None, :] * o
        xn2 = _ln(x) * (1 + sc_mlp[:, None, :]) + sh_mlp[:, None, :]
        h = jax.nn.gelu(xn2 @ w1 + b1, approximate=True)
        x = x + g_mlp[:, None, :] * (h @ w2 + b2)
        return x

    def _L1_cond_ref(x, c, W_qkv, b_qkv, W_proj, b_proj, W_fc1, b_fc1, W_fc2, b_fc2, W_ada, b_ada):
        import jax, jax.numpy as jnp
        import numpy as np
        B, L, C = (8, 256, 288)
        H = 16
        D = C // H
        FF = int(C * 4.0)
        EPS = 1e-06

        def _layernorm(x):
            mu = jnp.mean(x, axis=-1, keepdims=True)
            var = jnp.mean(jnp.square(x - mu), axis=-1, keepdims=True)
            return (x - mu) * jax.lax.rsqrt(var + EPS)

        def _modulate(x, shift, scale):
            return x * (1.0 + scale) + shift

        def _attention(h, W_qkv, b_qkv, W_proj, b_proj):
            b, l, c = h.shape
            qkv = h @ W_qkv + b_qkv
            qkv = qkv.reshape(b, l, 3, H, D)
            q, k, v = (qkv[:, :, 0], qkv[:, :, 1], qkv[:, :, 2])
            scale = D ** (-0.5)
            scores = jnp.einsum('blhd,bmhd->bhlm', q * scale, k)
            attn = jax.nn.softmax(scores, axis=-1)
            o = jnp.einsum('bhlm,bmhd->blhd', attn, v).reshape(b, l, c)
            return o @ W_proj + b_proj
        ada = jax.nn.silu(c) @ W_ada + b_ada
        shift_msa, scale_msa, gate_msa, shift_mlp, scale_mlp, gate_mlp = jnp.split(ada, 6, axis=-1)
        h = _modulate(_layernorm(x), shift_msa, scale_msa)
        x = x + gate_msa * _attention(h, W_qkv, b_qkv, W_proj, b_proj)
        h = _modulate(_layernorm(x), shift_mlp, scale_mlp)
        mlp = jax.nn.gelu(h @ W_fc1 + b_fc1, approximate=True) @ W_fc2 + b_fc2
        x = x + gate_mlp * mlp
        return x
    x = _L0_cond_ref(x, cond_1152, L0_cond_w_mod, L0_cond_b_mod, L0_cond_w_qkv, L0_cond_b_qkv, L0_cond_g_q, L0_cond_g_k, L0_cond_w_proj, L0_cond_b_proj, L0_cond_w1, L0_cond_b1, L0_cond_w2, L0_cond_b2)
    x = _L1_cond_ref(x, cond_1152[:, None, :], L1_cond_W_qkv, L1_cond_b_qkv, L1_cond_W_proj, L1_cond_b_proj, L1_cond_W_fc1, L1_cond_b_fc1, L1_cond_W_fc2, L1_cond_b_fc2, L1_cond_W_ada, L1_cond_b_ada)
    return x

_drawn_inputs = setup_inputs


def setup_inputs(seed=0):
    import zlib

    import numpy as np

    out = dict(_drawn_inputs(seed))
    spreads = {'L0_cond_b_qkv': (0.0, 0.378),
     'L0_cond_g_q': (1.0, 0.6),
     'L0_cond_g_k': (1.0, 0.6),
     'L0_cond_b_proj': (0.0, 0.391),
     'L0_cond_b1': (0.0, 0.506),
     'L0_cond_b2': (0.0, 0.416),
     'L1_cond_b_qkv': (0.0, 0.8),
     'L1_cond_b_proj': (0.0, 0.358),
     'L1_cond_b_fc1': (0.0, 0.8),
     'L1_cond_b_fc2': (0.0, 0.36),
     'L1_cond_b_ada': (0.0, 0.382)}
    factors = {'L0_cond_b_mod': 5.005, 'L1_cond_W_qkv': 7.94, 'L1_cond_W_proj': 5.205}
    for name, (base, spread) in spreads.items():
        noise = np.random.default_rng([zlib.crc32(name.encode()), seed]).standard_normal(out[name].shape)
        drawn = base * np.exp(spread * noise) if base else spread * noise
        out[name] = jnp.asarray(drawn.astype(out[name].dtype))
    for name, factor in factors.items():
        out[name] = (out[name] * factor).astype(out[name].dtype)
    return out
```

```python
from contextlib import ExitStack

import concourse.bass as bass
from concourse import mybir

ACT = mybir.ActivationFunctionType
ALU = mybir.AluOpType
AX = mybir.AxisListType
F32 = mybir.dt.float32
F32R = mybir.dt.float32r
I32 = mybir.dt.int32
ds = bass.ds

P = 128
B, L, C = 128, 64, 288
NH, HD = 16, 18
FF = 4 * C
T = B * L // P
SEQS = P // L
EPS = 1e-6
REST = C - 2 * P
BIAS = 3 * REST
SLOT = 64
PAIRS = NH // 2
HALF = NH // 2 * HD
QKVH = 3 * HALF
VW = HD + 1
GROUP = 4
GT = GROUP * P
GS = GROUP * SEQS
MT = FF // P
GUESS = float(0x5F3759DF - (1 << 22) - (1 << 30))
PICK, ONES = P + GT, P + GT + 1
SHIFT_MSA, SCALE_MSA, GATE_MSA, SHIFT_MLP, SCALE_MLP, GATE_MLP = range(6)


def wait(eng, sem, value):
    if not isinstance(value, int) or value > 0:
        eng.wait_ge(sem, value)


def steps(eng, emit, first, last, extra):
    for i in range(first):
        emit(i, i % 2)
    with eng.Fori(first // 2, last // 2) as r:
        for u in range(2):
            emit(2 * r + u, u)
    for i in range(last, last + extra):
        emit(i, i % 2)


def wait_apart(eng, idle, column, sem, value):
    eng.wait_ge(sem, value)
    eng.tensor_tensor(idle[:, column:column + 1], idle[:, 0:1], idle[:, 0:1], ALU.mult)


def within(t, n):
    return not isinstance(t, int) or 0 <= t < n


class Kit:

    def __init__(self, nc, ctx, prefix):
        self.nc, self.ctx, self.prefix, self.sems = nc, ctx, prefix, []
        ctx.callback(self.clear)

    def sb(self, name, shape, dt=F32):
        return self.ctx.enter_context(self.nc.sbuf_tensor(self.prefix + name, shape, dt))

    def ps(self, name, shape):
        return self.ctx.enter_context(self.nc.psum_tensor(self.prefix + name, shape, F32))

    def sem(self, name):
        made = self.nc.alloc_semaphore(self.prefix + name)
        self.sems.append(made)
        return made

    def clear(self):
        if self.sems:
            self.nc.clear_and_free_semaphores(self.sems)
            self.nc.all_engine_barrier()


def chunk_rows(c):
    return P if c < 2 else REST


def parity_count(t, parity, each):
    return each // 2 * (t - parity) + each


def three(pe, out, banks, n, acts, weights, rest_rows):
    (a_hi, a_lo, a_rest), (w_hi, w_lo, w_rest) = acts, weights
    for bank in range(banks):
        cols, dst = slice(bank * n, (bank + 1) * n), out[:, bank, 0:n]
        pe.matmul(dst, a_rest[0:rest_rows, :], w_rest[0:rest_rows, cols], start=True, stop=False)
        for c in range(2):
            pe.matmul(dst, a_hi[:, c, :], w_hi[:, c, cols], start=False, stop=False)
            pe.matmul(dst, a_hi[:, c, :], w_lo[:, c, cols], start=False, stop=False)
            last = pe.matmul(dst, a_lo[:, c, :], w_hi[:, c, cols], start=False, stop=(c == 1))
    return last


def transposes(pe, out, tile, rest, ident):
    pe.transpose(out[:, 0:P], tile[:, 0:P], ident[:, :])
    pe.transpose(out[:, P:2 * P], tile[:, P:2 * P], ident[:, :])
    return pe.transpose(out[:, 2 * P:3 * P], rest, ident[:, :])


def normalise(eng, xn, x, mv, rs, t):
    mean, rstd = mv[:, ds(t, 1), 0], rs[:, ds(t, 1)]
    eng.tensor_scalar(xn[:, 0:2 * P].unsqueeze(1), x[:, ds(t, 1), 0:2 * P], mean, rstd, ALU.subtract, ALU.mult)
    return eng.tensor_scalar(xn[:, 2 * P:3 * P].rearrange("p (a r) -> p a r", a=4), x[:, ds(t, 1), 2 * P:C].broadcast_to([P, 4, REST]),
                             mean, rstd, ALU.subtract, ALU.mult)


PT_BANK, XT_BANK, QT_BANK, OT_BANK, KT_BANK = (0, 1), 0, (1, 0), 1, (0, 1)


def modulation(nc, w, res, dram):
    with ExitStack() as ctx:
        k = Kit(nc, ctx, "mod_")
        cond = k.sb("cond", [P, C])
        ex = k.sb("ex", [P, C])
        den = k.sb("den", [P, C])
        rec = k.sb("rec", [P, C])
        silu = k.sb("silu", [P, C])
        condT = k.sb("condT", [P, 3, P])
        wm = k.sb("wm", [P, 3, 6 * C])
        wm_rest = k.sb("wm_rest", [P, 3, 4, P])
        gates = k.sb("gates", [P, 2, C])
        bn = k.sb("bn", [P, 2, 6])
        tr = k.ps("tr", [P, 3, P])
        feat = [k.ps(f"feat{i}", [P, 3, P]) for i in range(2)]
        gps = [k.ps(f"gps{i}", [P, C]) for i in range(2)]
        cond_in, x_in, ident_in = k.sem("cond_in"), [k.sem(f"x_in{i}") for i in range(8)], k.sem("ident_in")
        w_in = [k.sem(f"w_in{i}") for i in range(2)]
        exp_done, add_done, rec_done, silu_done = k.sem("exp"), k.sem("add"), k.sem("rec"), k.sem("silu")
        tr_done, condT_done = k.sem("tr_done"), k.sem("condT_done")
        feat_done, feat_read = k.sem("feat_done"), k.sem("feat_read")
        gate_done, gate_read, gate_out = k.sem("gate_done"), k.sem("gate_read"), k.sem("gate_out")
        bn_done, var_done, ones_done = k.sem("bn_done"), k.sem("var_done"), k.sem("ones_done")
        oh_in, rs_done, dup_done = k.sem("oh_in"), k.sem("rs_done"), k.sem("dup_done")
        ADAPT = [(SCALE_MSA, 1.0), (SHIFT_MSA, 0.0), (SCALE_MLP, 1.0), (SHIFT_MLP, 0.0)]

        with nc.Block() as block:

            @block.sync
            def _(sp):
                sp.dma_start(cond[:, :], w["cond_1152"]).then_inc(cond_in, 16)
                sp.dma_start(res["ident"][:, :], w["ident"]).then_inc(ident_in, 16)
                for l in range(2):
                    if l:
                        sp.wait_ge(feat_done, 4)
                        sp.wait_ge(gate_done, 2)
                    wmod, bmod = w[f"mod_w{l}"], w[f"mod_b{l}"]
                    for c in range(2):
                        sp.dma_start(wm[:, c, :], wmod[c * P:(c + 1) * P, :]).then_inc(w_in[l], 16)
                    sp.dma_start(wm[0:REST, 2, :], wmod[2 * P:C, :]).then_inc(w_in[l], 16)
                    sp.dma_start(wm[REST:REST + 1, 2, :], bmod).then_inc(w_in[l], 16)
                    if not l:
                        for n in range(8):
                            sp.dma_start(res["x"][:, 8 * n:8 * n + 8, :],
                                         w["x"][8 * n:8 * n + 8].rearrange("t p c -> p t c")).then_inc(x_in[n], 16)
                        sp.dma_start(res["hot"][BIAS:BIAS + 2 * GS, :], w["hot"]).then_inc(oh_in, 16)
                        sp.dma_start(res["hot"][0:2, :], w["hot"][0:2, :]).then_inc(oh_in, 16)
                sp.wait_ge(oh_in, 32)

            @block.scalar
            def _(act):
                act.wait_ge(ident_in, 16)
                act.activation(res["ident_r"][:, :], res["ident"][:, :], ACT.Copy)
                act.wait_ge(cond_in, 16)
                act.activation(ex[:, :], cond[:, :], ACT.Exp, scale=-1.0).then_inc(exp_done, 1)
                act.wait_ge(tr_done, 3)
                act.activation(condT[:, 0:2, :], tr[:, 0:2, :], ACT.Copy).then_inc(condT_done, 1)
                act.activation(condT[0:REST, 2, :], tr[0:REST, 2, :], ACT.Copy).then_inc(condT_done, 1)
                for l in range(2):
                    for g in range(2):
                        act.wait_ge(gate_done, 2 * l + g + 1)
                        if l:
                            act.wait_ge(gate_out, 32)
                        act.activation(gates[:, g, :], gps[g][:, :], ACT.Copy).then_inc(gate_read, 1)
                    for g in range(2):
                        act.wait_ge(gate_read, 2 * l + g + 1)
                        act.dma_start(dram[f"gate{l}{g}"], gates[:, g, :]).then_inc(gate_out, 16)
                act.wait_ge(gate_out, 64)

            @block.tensor
            def _(pe):
                pe.wait_ge(ident_in, 16)
                pe.wait_ge(silu_done, 1)
                for c in range(3):
                    n = chunk_rows(c)
                    pe.transpose(tr[0:n, c, :], silu[:, c * P:c * P + n], res["ident"][:, :]).then_inc(tr_done, 1)
                pe.wait_ge(condT_done, 2)
                pe.wait_ge(ones_done, 1)
                for l in range(2):
                    pe.wait_ge(w_in[l], 64)
                    for g, part in enumerate((GATE_MSA, GATE_MLP)):
                        wait(pe, gate_read, 2 * (l - 1) + g + 1)
                        for c in range(3):
                            n = P if c < 2 else REST + 1
                            mm = pe.matmul(gps[g][:, :], condT[0:n, c, :], wm[0:n, c, part * C:(part + 1) * C],
                                           start=(c == 0), stop=(c == 2))
                        mm.then_inc(gate_done, 1)
                    pe.wait_ge(dup_done, l + 1)
                    for j, (part, _) in enumerate(ADAPT):
                        m = 4 * l + j
                        wait(pe, feat_read, m - 1)
                        for o in range(3):
                            for c in range(3):
                                n = P if c < 2 else REST + 1
                                cols = wm[0:n, c, part * C + o * P:part * C + (o + 1) * P] if o < 2 else wm_rest[0:n, c, j, :]
                                mm = pe.matmul(feat[m % 2][:, o, :], cols, condT[0:n, c, :],
                                               start=(c == 0), stop=(c == 2))
                        mm.then_inc(feat_done, 1)

            @block.vector
            def _(dve):
                dve.memset(condT[REST:REST + 1, 2, :], 1.0).then_inc(ones_done, 1)
                dve.wait_ge(exp_done, 1)
                dve.tensor_scalar(den[:, :], ex[:, :], 1.0, None, ALU.add).then_inc(add_done, 1)
                dve.wait_ge(add_done, 1)
                dve.reciprocal(rec[:, :], den[:, :]).then_inc(rec_done, 1)
                dve.wait_ge(rec_done, 1)
                dve.tensor_tensor(silu[:, :], cond[:, :], rec[:, :], ALU.mult).then_inc(silu_done, 1)
                for l in range(2):
                    for j, (part, plus) in enumerate(ADAPT):
                        m = 4 * l + j
                        dve.wait_ge(feat_done, m + 1)
                        dst = res[f"adapt{l}{part}"]
                        dve.tensor_scalar(dst[:, :, :], feat[m % 2][:, :, :], plus, None, ALU.add).then_inc(feat_read, 1)
                        if part in (SHIFT_MSA, SHIFT_MLP):
                            dve.wait_ge(feat_read, m + 1)
                            dve.memset(dst[REST:REST + 1, 2, :], 1.0)
                for t in range(T):
                    if t % 8 == 0:
                        dve.wait_ge(x_in[t // 8], 16)
                    wait(dve, bn_done, 2 * (t - 1))
                    dve.bn_stats(bn[:, t % 2, :], res["x"][:, t, :]).then_inc(bn_done, 1)
                    dve.wait_ge(bn_done, 2 * t + 1)
                    dve.bn_aggr(res["mv"][:, t, :], bn[:, t % 2, :]).then_inc(bn_done, 1)
                dve.wait_ge(bn_done, 2 * T)
                dve.tensor_scalar(res["ve"][:, :], res["mv"][:, :, 1], EPS, None, ALU.add).then_inc(var_done, 1)

            @block.gpsimd
            def _(pool):
                pool.memset(res["mhalf"][:, :], -0.5).then_inc(rs_done, 1)
                for l in range(2):
                    pool.wait_ge(w_in[l], 64)
                    if l:
                        pool.wait_ge(feat_done, 4)
                    for j, (part, _) in enumerate(ADAPT):
                        for n, c in ((P, slice(0, 2)), (REST + 1, slice(2, 3))):
                            src = wm[0:n, c, part * C + 2 * P:(part + 1) * C]
                            last = pool.tensor_copy(wm_rest[0:n, c, j, :].rearrange("p c (a r) -> p c a r", a=4),
                                                    src.unsqueeze(2).broadcast_to([n, src.shape[1], 4, REST]))
                    last.then_inc(dup_done, 1)
                pool.wait_ge(rs_done, 1)
                pool.wait_ge(var_done, 1)
                pool.tensor_tensor(res["rs"][:, :], res["ve"][:, :], res["mhalf"][:, :], ALU.pow).then_inc(rs_done, 1)


def attention(nc, w, res, dram, l):
    with ExitStack() as ctx:
        k = Kit(nc, ctx, f"att{l}_")
        wqkv_hi, wqkv_lo = k.sb("wqkv_hi", [P, 2, 2 * QKVH], F32R), k.sb("wqkv_lo", [P, 2, 2 * QKVH], F32R)
        wqkv_rest = [k.sb(f"wqkv_rest{u}", [P, 2 * QKVH], F32R) for u in range(2)]
        wo_hi, wo_lo, wo_rest = k.sb("wo_hi", [P, 2, C], F32R), k.sb("wo_lo", [P, 2, C], F32R), k.sb("wo_rest", [P, C], F32R)
        gains = k.sb("gains", [P, HD])
        attention_weights(nc, w, res, dram, l, wqkv_hi, wqkv_lo, wqkv_rest, wo_hi, wo_lo, wo_rest, gains)
        attention_tiles(nc, w, res, dram, l, wqkv_hi, wqkv_lo, wqkv_rest, wo_hi, wo_lo, wo_rest, gains)


def attention_weights(nc, w, res, dram, l, wqkv_hi, wqkv_lo, wqkv_rest, wo_hi, wo_lo, wo_rest, gains):
    with ExitStack() as ctx:
        k = Kit(nc, ctx, f"aw{l}_")
        raw = k.sb("raw", [P, 3, 2 * QKVH])
        oraw = k.sb("oraw", [P, 3, C])
        obias, obias_hi = k.sb("obias", [P, C]), k.sb("obias_hi", [P, C], F32R)
        means = k.sb("means", [P, 3, 4 * 8])
        rows_hi, rows_lo = k.sb("rows_hi", [P, 2, QKVH], F32R), k.sb("rows_lo", [P, 2, QKVH], F32R)
        gq = k.sb("gq", [P, 2, HD])
        rps = k.ps("rps", [P, 2, 512])
        w_in, o_in, g_in = k.sem("w_in"), k.sem("o_in"), k.sem("g_in")
        mean_done, ready = k.sem("mean_done"), k.sem("ready")
        hi_done, lo_done, ohi_done, rows_done, rhi_done, rlo_done, rows_out = (
            k.sem(n) for n in ("hi", "lo", "ohi", "rows", "rhi", "rlo", "rows_out"))
        shift = res[f"adapt{l}{SHIFT_MSA}"]
        BLOCKS = [(P, slice(0, 2)), (REST + 1, slice(2, 3))]
        with nc.Block() as block:

            @block.sync
            def _(sp):
                wq, bq = w[f"qkv_w{l}"], w[f"qkv_b{l}"]
                for n in range(2):
                    for s in range(3):
                        src = slice(s * C + n * HALF, s * C + (n + 1) * HALF)
                        dst = slice(n * QKVH + s * HALF, n * QKVH + (s + 1) * HALF)
                        sp.dma_start(raw[:, 0:2, dst], wq[0:2 * P, src].rearrange("(c p) n -> p c n", c=2)).then_inc(w_in, 16)
                        sp.dma_start(raw[0:REST, 2, dst], wq[2 * P:C, src]).then_inc(w_in, 16)
                        sp.dma_start(raw[REST:REST + 1, 2, dst], bq[:, src]).then_inc(w_in, 16)
                wo, bo = w[f"o_w{l}"], w[f"o_b{l}"]
                sp.dma_start(oraw[:, 0:2, :], wo[0:2 * P, :].rearrange("(c p) n -> p c n", c=2)).then_inc(o_in, 16)
                sp.dma_start(oraw[0:REST, 2, :], wo[2 * P:C, :]).then_inc(o_in, 16)
                sp.dma_start(obias[BIAS:BIAS + 2, :], bo.broadcast_to([2, C])).then_inc(o_in, 16)
                if l == 0:
                    for s in range(2):
                        sp.dma_start(gq[:, s, :], w[f"gain{s}"].broadcast_to([P, HD])).then_inc(g_in, 16)
                for n, (done, rows) in enumerate(((rhi_done, rows_hi), (rlo_done, rows_lo))):
                    sp.wait_ge(done, 1)
                    sp.dma_start(dram[f"qkv_rows{l}"][n], rows[:, :, :].rearrange("p a b -> p (a b)").bitcast(F32)).then_inc(rows_out, 16)
                sp.wait_ge(rows_out, 32)

            @block.vector
            def _(dve):
                dve.wait_ge(w_in, 9 * 2 * 16)
                if l == 0:
                    for i, (rows, c) in enumerate(BLOCKS):
                        nchunk = c.stop - c.start
                        heads = [raw[0:rows, c, n * QKVH:n * QKVH + 2 * HALF].rearrange("p c (h d) -> p c h d", d=HD) for n in range(2)]
                        for n in range(2):
                            mean = means[0:rows, c, 16 * n:16 * n + 16]
                            dve.tensor_reduce(mean, heads[n], AX.X, ALU.add).then_inc(mean_done, 1)
                            dve.wait_ge(mean_done, 3 * (2 * i + n) + 1)
                            dve.tensor_scalar(mean, mean, 1.0 / HD, None, ALU.mult).then_inc(mean_done, 1)
                            dve.wait_ge(mean_done, 3 * (2 * i + n) + 2)
                            for cc in range(nchunk):
                                last = dve.tensor_tensor(heads[n][:, cc], heads[n][:, cc],
                                                         mean[:, cc].unsqueeze(2).broadcast_to([rows, 16, HD]), ALU.subtract)
                            last.then_inc(mean_done, 1)
                    dve.wait_ge(g_in, 32)
                    dve.tensor_scalar(gq[:, 0, :], gq[:, 0, :], float(HD) ** -0.5, None, ALU.mult).then_inc(mean_done, 1)
                    dve.wait_ge(mean_done, 13)
                    dve.tensor_tensor(gains[:, :], gq[:, 0, :], gq[:, 1, :], ALU.mult).then_inc(ready, 1)
                else:
                    for rows, c in BLOCKS:
                        for n in range(2):
                            kcols = raw[0:rows, c, n * QKVH + HALF:n * QKVH + 2 * HALF]
                            last = dve.tensor_scalar(kcols, kcols, float(HD) ** -0.5, None, ALU.mult)
                    last.then_inc(ready, 1)
                dve.wait_ge(hi_done, 3)
                dve.tensor_tensor(wqkv_lo[:, :, :], raw[:, 0:2, :], wqkv_hi[:, :, :], ALU.subtract).then_inc(lo_done, 1)
                for u in range(2):
                    dve.tensor_tensor(wqkv_rest[u][2 * REST:3 * REST, :], raw[0:REST, 2, :], wqkv_rest[u][0:REST, :],
                                      ALU.subtract).then_inc(lo_done, 1)
                dve.wait_ge(ohi_done, 4)
                dve.tensor_tensor(wo_lo[:, :, :], oraw[:, 0:2, :], wo_hi[:, :, :], ALU.subtract).then_inc(lo_done, 1)
                dve.tensor_tensor(wo_rest[2 * REST:3 * REST, :], oraw[0:REST, 2, :], wo_rest[0:REST, :], ALU.subtract).then_inc(lo_done, 1)
                dve.scalar_tensor_tensor(wo_rest[BIAS:BIAS + 2, :], obias_hi[BIAS:BIAS + 2, :], res["hot"][BIAS:BIAS + 2, PICK:PICK + 1],
                                         obias[BIAS:BIAS + 2, :], ALU.mult, ALU.add).then_inc(lo_done, 1)
                dve.wait_ge(rhi_done, 1)
                dve.tensor_tensor(rows_lo[:, :, :], rps[:, :, 0:QKVH], rows_hi[:, :, :], ALU.subtract).then_inc(rlo_done, 1)

            @block.scalar
            def _(act):
                act.wait_ge(o_in, 48)
                act.activation(wo_hi[:, :, :], oraw[:, 0:2, :], ACT.Copy).then_inc(ohi_done, 1)
                act.activation(wo_rest[0:REST, :], oraw[0:REST, 2, :], ACT.Copy).then_inc(ohi_done, 1)
                act.activation(wo_rest[REST:2 * REST, :], oraw[0:REST, 2, :], ACT.Copy).then_inc(ohi_done, 1)
                act.activation(obias_hi[BIAS:BIAS + 2, :], obias[BIAS:BIAS + 2, :], ACT.Copy).then_inc(ohi_done, 1)
                act.wait_ge(ready, 1)
                act.activation(wqkv_hi[:, :, :], raw[:, 0:2, :], ACT.Copy).then_inc(hi_done, 1)
                for u in range(2):
                    act.activation(wqkv_rest[u][0:REST, :], raw[0:REST, 2, :], ACT.Copy)
                    act.activation(wqkv_rest[u][REST:2 * REST, :], raw[0:REST, 2, :], ACT.Copy).then_inc(hi_done, 1)
                act.wait_ge(rows_done, 1)
                act.activation(rows_hi[:, :, :], rps[:, :, 0:QKVH], ACT.Copy).then_inc(rhi_done, 1)

            @block.tensor
            def _(pe):
                pe.wait_ge(ready, 1)
                for n in range(2):
                    for c in range(3):
                        kk = P if c < 2 else REST + 1
                        mm = pe.matmul(rps[:, n, 0:QKVH], shift[0:kk, c, :], raw[0:kk, c, n * QKVH:(n + 1) * QKVH],
                                       start=(c == 0), stop=(c == 2))
                mm.then_inc(rows_done, 1)


def attention_tiles(nc, w, res, dram, l, wqkv_hi, wqkv_lo, wqkv_rest, wo_hi, wo_lo, wo_rest, gains):
    with ExitStack() as ctx:
        k = Kit(nc, ctx, f"at{l}_")
        normed = lambda: l == 0
        xn = k.sb("xn", [P, 3 * P])
        xs = k.sb("xs", [P, 3, P])
        x_hi, x_lo, x_rest = k.sb("x_hi", [P, 2, P], F32R), k.sb("x_lo", [P, 2, P], F32R), k.sb("x_rest", [P, P], F32R)
        qk = k.sb("qk", [P, 2, 2, 8, HD])
        sq = k.sb("sq", [P, 2, 16 * HD])
        ss, vh, y0, t0, t1, three_halves = (k.sb(n, [P, 32]) for n in ("ss", "vh", "y0", "t0", "t1", "three_halves"))
        stack = k.sb("stack", [P, 2, 2, 8, SLOT], F32R)
        vals = [k.sb(f"vals{u}", [P, SEQS, NH, VW]) for u in range(2)]
        qT = k.sb("qT", [P, PAIRS, SEQS, 2, L], F32R)
        kT = k.sb("kT", [P, PAIRS, SEQS, L], F32R)
        mx = k.sb("mx", [P, 16])
        sd = k.sb("sd", [P, 16, L])
        pr = k.sb("pr", [P, 16, L])
        prT = k.sb("prT", [P, PAIRS, P])
        rc = k.sb("rc", [P, 2, 16])
        idle_pool, idle_dve = k.sb("idle_pool", [P, 8]), k.sb("idle_dve", [P, 8])
        o = k.sb("o", [P, NH, HD])
        o_dup = k.sb("o_dup", [P, P])
        o_hi, o_lo, o_rest = k.sb("o_hi", [P, 2, P], F32R), k.sb("o_lo", [P, 2, P], F32R), k.sb("o_rest", [P, P], F32R)
        gate = [k.sb(f"gate{u}", [P, C]) for u in range(2)]
        upd = k.sb("upd", [P, C])
        bn, mv = k.sb("bn", [P, 6]), k.sb("mv", [P, 2])
        tp, qp, sp_, op = (k.ps(n, [P, 2, 512]) for n in ("tp", "qp", "sp", "op"))
        s = {n: k.sem(n) for n in (
            "started", "zero", "init", "xn", "xT", "xs", "xhi", "xlo", "qkv", "sq", "ss", "vh", "rr", "qk", "kg", "khi", "vals", "klo", "kdup",
            "qTt", "kTt", "qTa", "qTd", "kTa", "kTd", "score", "mx", "sub", "exp", "prT", "prTe", "pv", "rc", "o", "odup",
            "oT", "ohi", "olo", "proj", "upd", "x", "bn", "ve", "rs", "nw")}
        rows_in = [k.sem(f"rows_in{u}") for u in range(2)]
        gate_in = [k.sem(f"gate_in{u}") for u in range(2)]
        FIRST, EXTRA = 4, 3
        scale = res[f"adapt{l}{SCALE_MSA}"]

        def split_view(bank_ap):
            return bank_ap[:, :, 0:2 * HALF].rearrange("p n (s h d) -> p n s h d", s=2, d=HD)

        with nc.Block() as block:

            @block.sync
            def _(sp):
                def emit(i, u):
                    if within(i, T):
                        wait(sp, s["qkv"], i - 1)
                        for n in range(2):
                            r = BIAS + SEQS * n
                            sp.dma_start(wqkv_rest[u][r:r + SEQS, :].bitcast(F32),
                                         dram[f"qkv_rows{l}"][n, ds(SEQS * i, SEQS), :]).then_inc(rows_in[u], 16)
                        wait(sp, s["upd"], i - 1)
                        for b in range(SEQS):
                            sp.dma_start(gate[u][b * L:(b + 1) * L, :],
                                         dram[f"gate{l}0"][ds(SEQS * i + b, 1), :].broadcast_to([L, C])).then_inc(gate_in[u], 16)
                steps(sp, emit, FIRST, T, 0)

            @block.gpsimd
            def _(pool):
                pool.memset(stack[:, :, :, :, 3 * HD:SLOT].bitcast(F32), 0.0).then_inc(s["init"], 1)
                pool.memset(qT[:, :, :, :, :].bitcast(F32), 0.0).then_inc(s["init"], 1)
                pool.memset(idle_pool[:, :], 0.0).then_inc(s["started"], 1)
                pool.memset(three_halves[:, :], 1.5).then_inc(s["started"], 1)
                pool.wait_ge(s["started"], 2)

                def emit(i, u):
                    if within(i - 1, T):
                        t = i - 1
                        if normed():
                            rsqrt(pool, t)
                            pool.wait_ge(s["qk"], t + 1)
                            for n in range(2):
                                last = pool.tensor_tensor(qk[:, n, 1], qk[:, n, 1],
                                                          gains[:, :].unsqueeze(1).broadcast_to([P, 8, HD]), ALU.mult)
                            last.then_inc(s["kg"], 1)
                        wait_apart(pool, idle_pool, 1, s["khi"], t + 1)
                        pool.tensor_copy(stack[:, :, 0, :, HD:2 * HD], stack[:, :, 0, :, 0:HD])
                        pool.tensor_copy(stack[:, :, 1, :, 2 * HD:3 * HD], stack[:, :, 1, :, 0:HD]).then_inc(s["kdup"], 1)
                    if within(i, T):
                        pool.wait_ge(s["xhi"], 2 * i + 2)
                        pool.tensor_tensor(x_lo[:, :, :], xs[:, 0:2, :], x_hi[:, :, :], ALU.subtract).then_inc(s["xlo"], 1)
                        pool.wait_ge(s["xlo"], 2 * i + 1)
                        pool.tensor_tensor(x_rest[REST:2 * REST, :], xs[REST:2 * REST, 2, :], x_rest[REST:2 * REST, :],
                                           ALU.subtract).then_inc(s["xlo"], 1)
                        pool.wait_ge(s["xlo"], 2 * i + 2)
                    if within(i - 2, T):
                        t = i - 2
                        wait(pool, s["oT"], t)
                        wait_apart(pool, idle_pool, 2, s["o"], t + 1)
                        pool.tensor_copy(o_dup[:, :].rearrange("p (a r) -> p a r", a=4),
                                         o[:, :, :].rearrange("p h d -> p (h d)")[:, 2 * P:C].unsqueeze(1).broadcast_to([P, 4, REST]))\
                            .then_inc(s["odup"], 1)
                        pool.wait_ge(s["upd"], t + 1)
                        pool.tensor_tensor(res["x"][:, ds(t, 1), :], res["x"][:, ds(t, 1), :], upd[:, :].unsqueeze(1), ALU.add)\
                            .then_inc(s["x"], 1)
                    if within(i - 3, T):
                        t = i - 3
                        pool.wait_ge(s["ve"], t + 1)
                        pool.tensor_tensor(res["rs"][:, ds(t, 1)], res["ve"][:, ds(t, 1)], res["mhalf"][:, 0:1], ALU.pow)\
                            .then_inc(s["rs"], 1)

                def rsqrt(pool, t):
                    STEPS = 12
                    pool.wait_ge(s["ss"], t + 1)
                    n = 0
                    for _ in range(3):
                        for out_, in0, in1, op_ in ((t0, y0, y0, ALU.mult), (t1, t0, vh, ALU.mult),
                                                    (t0, t1, three_halves, ALU.add), (y0, y0, t0, ALU.mult)):
                            if n:
                                pool.wait_ge(s["nw"], STEPS * t + n)
                            pool.tensor_tensor(out_[:, :], in0[:, :], in1[:, :], op_).then_inc(s["nw"], 1)
                            n += 1
                steps(pool, emit, FIRST, T, EXTRA)
                pool.wait_ge(s["rs"], T)

            @block.vector
            def _(dve):
                dve.memset(idle_dve[:, :], 0.0).then_inc(s["zero"], 1)
                for v in vals:
                    dve.memset(v[:, :, :, :], 0.0).then_inc(s["zero"], 1)
                dve.wait_ge(s["zero"], 3)
                for v in vals:
                    for b in range(SEQS):
                        dve.memset(v[b * L:(b + 1) * L, b, :, HD:VW], 1.0).then_inc(s["init"], 1)

                def emit(i, u):
                    if within(i, T):
                        wait(dve, s["xT"], i)
                        normalise(dve, xn, res["x"], res["mv"], res["rs"], i).then_inc(s["xn"], 1)
                    t = i - 2
                    if within(t, T):
                        for n in range(2):
                            dve.wait_ge(s["score"], 2 * t + n + 1)
                            dve.tensor_reduce(mx[:, 8 * n:8 * n + 8], sp_[:, n, :].rearrange("p (h q) -> p h q", h=8),
                                              AX.X, ALU.max).then_inc(s["mx"], 1)
                            dve.wait_ge(s["mx"], 2 * t + n + 1)
                            wait(dve, s["exp"], 2 * t + n - 1)
                            dve.tensor_tensor(sd[:, 8 * n:8 * n + 8, :], sp_[:, n, :].rearrange("p (h q) -> p h q", h=8),
                                              mx[:, 8 * n:8 * n + 8].unsqueeze(2).broadcast_to([P, 8, L]),
                                              ALU.subtract).then_inc(s["sub"], 1)
                    t = i - 1
                    if within(t, T):
                        if normed():
                            dve.wait_ge(s["sq"], t + 1)
                            wait(dve, s["qk"], t)
                            dve.tensor_reduce(ss[:, :].rearrange("p (n h) -> p n h", n=2),
                                              sq[:, :, :].rearrange("p n (h d) -> p n h d", d=HD), AX.X, ALU.add)\
                                .then_inc(s["rr"], 1)
                            dve.wait_ge(s["rr"], t + 1)
                            dve.tensor_scalar(vh[:, :], ss[:, :], -0.5 / HD, -0.5 * EPS, ALU.mult, ALU.add).then_inc(s["vh"], 1)
                            dve.wait_ge(s["vh"], t + 1)
                            dve.tensor_scalar(y0[:, :].bitcast(I32), vh[:, :].bitcast(I32), -0.5, GUESS, ALU.mult, ALU.add).then_inc(s["ss"], 1)
                            dve.wait_ge(s["nw"], 12 * t + 12)
                            dve.wait_ge(s["vals"], t + 1)
                            wait(dve, s["klo"], t)
                            for n in range(2):
                                last = dve.tensor_tensor(
                                    qk[:, n].rearrange("p s h d -> p (s h) d"),
                                    qp[:, n, 0:2 * HALF].rearrange("p (h d) -> p h d", d=HD),
                                    y0[:, 16 * n:16 * n + 16].unsqueeze(2).broadcast_to([P, 16, HD]), ALU.mult)
                            last.then_inc(s["qk"], 1)
                    if within(i, T):
                        dve.wait_ge(s["xT"], i + 1)
                        wait(dve, s["xlo"], 2 * i)
                        b = scale[:, :, ds(SEQS * i, SEQS)].unsqueeze(3).broadcast_to([P, 3, SEQS, L])
                        dve.tensor_tensor(xs[:, :, :].rearrange("p c (b q) -> p c b q", b=SEQS),
                                          tp[:, XT_BANK, 0:3 * P].rearrange("p (c b q) -> p c b q", c=3, b=SEQS), b,
                                          ALU.mult).then_inc(s["xs"], 1)
                    if within(t, T):
                        dve.wait_ge(s["khi"], t + 1)
                        dve.wait_ge(s["vals"], t + 1)
                        src = [qk[:, :, j] if normed() else split_view(qp[:, :, :])[:, :, j] for j in range(2)]
                        if normed():
                            dve.wait_ge(s["kg"], t + 1)
                        dve.tensor_tensor(stack[:, :, 0, :, 2 * HD:3 * HD], src[0], stack[:, :, 0, :, 0:HD], ALU.subtract)
                        dve.tensor_tensor(stack[:, :, 1, :, HD:2 * HD], src[1], stack[:, :, 1, :, 0:HD], ALU.subtract)\
                            .then_inc(s["klo"], 1)
                    t = i - 2
                    if within(t, T):
                        dve.wait_ge(s["pv"], t + 1)
                        dve.reciprocal(rc[:, :, :], op[:, :, 0:16 * VW].rearrange("p n (g v) -> p n g v", v=VW)[:, :, :, HD])\
                            .then_inc(s["rc"], 1)
                        dve.wait_ge(s["rc"], t + 1)
                        wait(dve, s["oT"], t)
                        for j in range(2):
                            for b in range(SEQS):
                                rows, dst = slice(j * L, (j + 1) * L), slice(b * L, (b + 1) * L)
                                src = op[rows, :, 0:16 * VW].rearrange("p n (g a v) -> p n g a v", g=4, v=VW)[:, :, :, 2 * b + j, 0:HD]
                                fac = rc[rows, :, :].rearrange("p n (g a) -> p n g a", g=4)[:, :, :, 2 * b + j]
                                last = dve.tensor_tensor(
                                    o[dst, :, :].rearrange("p (n g j) d -> p n g j d", n=2, j=2)[:, :, :, j, :], src,
                                    fac.unsqueeze(3).broadcast_to([L, 2, 4, HD]), ALU.mult)
                        last.then_inc(s["o"], 1)
                    t = i - 1
                    if within(t, T):
                        for n in range(2):
                            dve.wait_ge(s["qTt"], 2 * t + n + 1)
                            if n == 0:
                                wait(dve, s["score"], 2 * t)
                            dve.tensor_copy(qT[L:P, 4 * n:4 * n + 4, :, 1, :],
                                            tp[L:P, QT_BANK[n], :].rearrange("p (g b q) -> p g b q", g=4, b=SEQS)).then_inc(s["qTd"], 1)
                    t = i - 2
                    if within(t, T):
                        dve.wait_ge(s["ohi"], 2 * t + 2)
                        dve.tensor_tensor(o_lo[:, :, :], tp[:, OT_BANK, 0:2 * P].rearrange("p (c q) -> p c q", c=2), o_hi[:, :, :],
                                          ALU.subtract)
                        dve.tensor_tensor(o_rest[REST:2 * REST, :], tp[REST:2 * REST, OT_BANK, 2 * P:3 * P],
                                          o_rest[REST:2 * REST, :], ALU.subtract).then_inc(s["olo"], 1)
                    t = i - 1
                    if within(t, T):
                        dve.wait_ge(s["kTt"], 2 * t + 2)
                        dve.tensor_copy(kT[:, 4:8, :, :],
                                        tp[:, KT_BANK[1], :].rearrange("p (g b q) -> p g b q", g=4, b=SEQS)).then_inc(s["kTd"], 1)
                    t = i - 2
                    if within(t, T):
                        dve.wait_ge(s["proj"], t + 1)
                        dve.wait_ge(gate_in[u], parity_count(t, u, 32))
                        wait(dve, s["x"], t)
                        dve.tensor_tensor(upd[:, :], op[:, 0, 0:C], gate[u][:, :], ALU.mult).then_inc(s["upd"], 1)
                    t = i - 3
                    if within(t, T):
                        dve.wait_ge(s["x"], t + 1)
                        dve.bn_stats(bn[:, :], res["x"][:, ds(t, 1), :]).then_inc(s["bn"], 1)
                        wait_apart(dve, idle_dve, 3, s["bn"], 2 * t + 1)
                        dve.bn_aggr(mv[:, :], bn[:, :]).then_inc(s["bn"], 1)
                        dve.wait_ge(s["bn"], 2 * t + 2)
                        dve.tensor_copy(res["mv"][:, ds(t, 1), 0], mv[:, 0:1])
                        dve.tensor_scalar(res["ve"][:, ds(t, 1)], mv[:, 1:2], EPS, None, ALU.add).then_inc(s["ve"], 1)
                steps(dve, emit, FIRST, T, EXTRA)

            @block.scalar
            def _(act):
                act.activation(x_rest[BIAS:BIAS + 2 * SEQS, :], res["hot"][BIAS:BIAS + 2 * SEQS, 0:P], ACT.Copy)
                act.activation(o_rest[BIAS:BIAS + 2, :], res["hot"][BIAS:BIAS + 2, ONES:], ACT.Copy).then_inc(s["init"], 1)
                act.wait_ge(s["init"], 7)

                def emit(i, u):
                    t = i - 2
                    if within(t, T):
                        for n in range(2):
                            act.wait_ge(s["sub"], 2 * t + n + 1)
                            wait(act, s["prT"], 2 * t + n - 1)
                            act.activation(pr[:, 8 * n:8 * n + 8, :], sd[:, 8 * n:8 * n + 8, :], ACT.Exp).then_inc(s["exp"], 1)
                    t = i - 1
                    if within(t, T):
                        act.wait_ge(s["qkv"], t + 1)
                        if normed():
                            wait(act, s["ss"], t)
                            act.activation(sq[:, :, :], qp[:, :, 0:2 * HALF], ACT.Square).then_inc(s["sq"], 1)
                        else:
                            wait(act, s["kTt"], 2 * t)
                            act.activation(stack[:, :, :, :, 0:HD].rearrange("p n s h d -> p n (s h) d"),
                                           qp[:, :, 0:2 * HALF].rearrange("p n (h d) -> p n h d", d=HD), ACT.Copy).then_inc(s["khi"], 1)
                        wait(act, s["pv"], t - 1)
                        for b in range(SEQS):
                            rows = slice(b * L, (b + 1) * L)
                            last = act.activation(vals[1 - u][rows, b, :, 0:HD].rearrange("p (n h) d -> p n h d", n=2),
                                                  qp[rows, :, 2 * HALF:QKVH].rearrange("p n (h d) -> p n h d", d=HD), ACT.Copy)
                        last.then_inc(s["vals"], 1)
                    t = i - 2
                    if within(t, T):
                        for n in range(2):
                            act.wait_ge(s["prT"], 2 * t + n + 1)
                            wait(act, s["pv"], t)
                            act.activation(prT[:, 4 * n:4 * n + 4, :], tp[:, PT_BANK[n], :].rearrange("p (g q) -> p g q", g=4),
                                           ACT.Copy).then_inc(s["prTe"], 1)
                    if within(i, T):
                        act.wait_ge(s["xs"], i + 1)
                        wait(act, s["qkv"], i)
                        act.activation(x_hi[:, :, :], xs[:, 0:2, :], ACT.Copy).then_inc(s["xhi"], 1)
                        act.activation(x_rest[0:BIAS, :], xs[0:BIAS, 2, :], ACT.Copy).then_inc(s["xhi"], 1)
                    t = i - 1
                    if within(t, T):
                        if normed():
                            act.wait_ge(s["kg"], t + 1)
                            wait(act, s["kTt"], 2 * t)
                            act.activation(stack[:, :, :, :, 0:HD].rearrange("p n s h d -> p n (s h) d"),
                                           qk[:, :, :, :, :].rearrange("p n s h d -> p n (s h) d"), ACT.Copy).then_inc(s["khi"], 1)
                        for n in range(2):
                            act.wait_ge(s["qTt"], 2 * t + n + 1)
                            if n == 0:
                                wait(act, s["score"], 2 * t)
                            act.activation(qT[0:L, 4 * n:4 * n + 4, :, 0, :],
                                           tp[0:L, QT_BANK[n], :].rearrange("p (g b q) -> p g b q", g=4, b=SEQS), ACT.Copy).then_inc(s["qTa"], 1)
                    t = i - 2
                    if within(t, T):
                        act.wait_ge(s["oT"], t + 1)
                        wait(act, s["proj"], t)
                        act.activation(o_hi[:, :, :], tp[:, OT_BANK, 0:2 * P].rearrange("p (c q) -> p c q", c=2), ACT.Copy).then_inc(s["ohi"], 1)
                        act.activation(o_rest[0:BIAS, :], tp[0:BIAS, OT_BANK, 2 * P:3 * P], ACT.Copy).then_inc(s["ohi"], 1)
                    t = i - 1
                    if within(t, T):
                        act.wait_ge(s["kTt"], 2 * t + 1)
                        act.activation(kT[:, 0:4, :, :],
                                       tp[:, KT_BANK[0], :].rearrange("p (g b q) -> p g b q", g=4, b=SEQS), ACT.Copy).then_inc(s["kTa"], 1)
                steps(act, emit, FIRST, T, EXTRA)

            @block.tensor
            def _(pe):
                ident, ident_r = res["ident"], res["ident_r"]

                def emit(i, u):
                    t = i - 1
                    if within(t, T):
                        pe.wait_ge(s["xhi"], 2 * t + 2)
                        pe.wait_ge(s["xlo"], 2 * t + 2)
                        pe.wait_ge(rows_in[1 - u], parity_count(t, 1 - u, 32))
                        wait(pe, s["klo"], t)
                        wait(pe, s["vals"], t)
                        three(pe, qp, 2, QKVH, (x_hi, x_lo, x_rest), (wqkv_hi, wqkv_lo, wqkv_rest[1 - u]), BIAS + 2 * SEQS)\
                            .then_inc(s["qkv"], 1)
                    t = i - 2
                    if within(t, T):
                        for n in range(2):
                            pe.wait_ge(s["exp"], 2 * t + n + 1)
                            if n == 0:
                                wait(pe, s["kTa"], t + 1)
                            else:
                                wait(pe, s["kTd"], t + 1)
                            for g in range(4):
                                p = 4 * n + g
                                last = pe.transpose(tp[:, PT_BANK[n], g * P:(g + 1) * P],
                                                    pr[:, 2 * p:2 * p + 2, :].rearrange("p b q -> p (b q)"), ident[:, :])
                            last.then_inc(s["prT"], 1)
                    if within(i, T):
                        pe.wait_ge(s["xn"], i + 1)
                        wait(pe, s["prTe"], 2 * (i - 2) + 1)
                        transposes(pe, tp[:, XT_BANK], xn, xn[:, 2 * P:3 * P], ident).then_inc(s["xT"], 1)
                    if within(t, T):
                        pe.wait_ge(s["prTe"], 2 * t + 2)
                        wait(pe, s["upd"], t)
                        for p in range(PAIRS):
                            last = pe.matmul(op[:, p // 4, (p % 4) * 4 * VW:(p % 4 + 1) * 4 * VW], prT[:, p, :],
                                             vals[u][:, :, 2 * p:2 * p + 2, :].rearrange("p b j v -> p b (j v)"),
                                             start=True, stop=True)
                        last.then_inc(s["pv"], 1)
                    t = i - 1
                    if within(t, T):
                        pe.wait_ge(s["klo"], t + 1)
                        pe.wait_ge(s["kdup"], t + 1)
                        wait(pe, s["prTe"], 2 * t)
                        stack_transposes(pe, 0, 0)
                        if within(i, T):
                            pe.wait_ge(s["xs"], i + 1)
                        stack_transposes(pe, 0, 1)
                    t = i - 2
                    if within(t, T):
                        pe.wait_ge(s["odup"], t + 1)
                        if within(t + 1, T):
                            pe.wait_ge(s["qTa"], 2 * (t + 1) + 1)
                            pe.wait_ge(s["qTd"], 2 * (t + 1) + 1)
                        transposes(pe, tp[:, OT_BANK], o[:, :, :].rearrange("p h d -> p (h d)"), o_dup[:, :], ident).then_inc(s["oT"], 1)
                    t = i - 1
                    if within(t, T):
                        pe.wait_ge(s["qTa"], 2 * t + 2)
                        pe.wait_ge(s["qTd"], 2 * t + 2)
                        stack_transposes(pe, 1, 0)
                        wait(pe, s["ohi"], 2 * (t - 1) + 2)
                        wait(pe, s["olo"], t)
                        stack_transposes(pe, 1, 1)
                    t = i - 2
                    if within(t, T):
                        pe.wait_ge(s["ohi"], 2 * t + 2)
                        pe.wait_ge(s["olo"], t + 1)
                        three(pe, op, 1, C, (o_hi, o_lo, o_rest), (wo_hi, wo_lo, wo_rest), BIAS + 2).then_inc(s["proj"], 1)
                    t = i - 1
                    if within(t, T):
                        pe.wait_ge(s["kTa"], t + 1)
                        pe.wait_ge(s["kTd"], t + 1)
                        wait(pe, s["sub"], 2 * t)
                        for p in range(PAIRS):
                            for b in range(SEQS):
                                c = (2 * p + b) % 8
                                last = pe.matmul(sp_[:, p // 4, c * L:(c + 1) * L],
                                                 qT[:, p, b, :, :].rearrange("p j q -> p (j q)"), kT[:, p, b, :], start=True, stop=True)
                            if p % 4 == 3:
                                last.then_inc(s["score"], 1)

                def stack_transposes(pe, j, n):
                    bank = (QT_BANK, KT_BANK)[j][n]
                    for g in range(4):
                        last = pe.transpose(tp[:, bank, g * P:(g + 1) * P].bitcast(F32R),
                                            stack[:, n, j, 2 * g:2 * g + 2, :].rearrange("p h r -> p (h r)"), ident_r[:, :])
                    last.then_inc(s["qTt" if j == 0 else "kTt"], 1)
                steps(pe, emit, FIRST, T, EXTRA)



def mlp(nc, w, res, dram, out, l):
    with ExitStack() as ctx:
        k = Kit(nc, ctx, f"mlp{l}_")
        w1 = k.sb("w1_hi", [P, 2, FF], F32R), k.sb("w1_lo", [P, 2, FF], F32R), [k.sb(f"w1_rest{u}", [P, FF], F32R) for u in range(2)]
        w2 = k.sb("w2_hi", [P, MT, C], F32R), k.sb("w2_lo", [P, MT, C], F32R)
        b2 = k.sb("b2", [2, C], F32R)
        mlp_weights(nc, w, res, dram, l, w1, w2, b2)
        mlp_groups(nc, res, dram, out, l, w1, w2, b2)


def mlp_weights(nc, w, res, dram, l, w1, w2, b2):
    w1_hi, w1_lo, w1_rest = w1
    w2_hi, w2_lo = w2
    BANKS, BN = 3, FF // 3
    with ExitStack() as ctx:
        k = Kit(nc, ctx, f"mw{l}_")
        raw = k.sb("raw", [P, 3, FF])
        raw2 = k.sb("raw2", [P, MT, C])
        braw, braw_hi = k.sb("braw", [2, C]), k.sb("braw_hi", [2, C], F32R)
        rows_hi, rows_lo = k.sb("rows_hi", [P, BANKS, BN], F32R), k.sb("rows_lo", [P, BANKS, BN], F32R)
        rps = k.ps("rps", [P, BANKS, 512])
        w_in, w2_in = k.sem("w_in"), k.sem("w2_in")
        hi_done, hi2_done, rows_done, rhi_done, rlo_done, rows_out = (
            k.sem(n) for n in ("hi", "hi2", "rows", "rhi", "rlo", "rows_out"))
        shift = res[f"adapt{l}{SHIFT_MLP}"]
        with nc.Block() as block:

            @block.sync
            def _(sp):
                w1d, w2d = w[f"fc1_w{l}"], w[f"fc2_w{l}"]
                for c in range(2):
                    sp.dma_start(raw[:, c, :], w1d[c * P:(c + 1) * P, :]).then_inc(w_in, 16)
                sp.dma_start(raw[0:REST, 2, :], w1d[2 * P:C, :]).then_inc(w_in, 16)
                sp.dma_start(raw[REST:REST + 1, 2, :], w[f"fc1_b{l}"]).then_inc(w_in, 16)
                sp.dma_start(raw2[:, :, :], w2d.rearrange("(m p) n -> p m n", p=P)).then_inc(w2_in, 16)
                sp.dma_start(braw[:, :], w[f"fc2_b{l}"].broadcast_to([2, C])).then_inc(w2_in, 16)
                for n, (done, rows) in enumerate(((rhi_done, rows_hi), (rlo_done, rows_lo))):
                    sp.wait_ge(done, 1)
                    sp.dma_start(dram[f"fc_rows{l}"][n], rows[:, :, :].rearrange("p a b -> p (a b)").bitcast(F32)).then_inc(rows_out, 16)
                sp.wait_ge(rows_out, 32)

            @block.scalar
            def _(act):
                act.wait_ge(w_in, 64)
                act.activation(w1_hi[:, :, :], raw[:, 0:2, :], ACT.Copy).then_inc(hi_done, 1)
                for u in range(2):
                    act.activation(w1_rest[u][0:REST, :], raw[0:REST, 2, :], ACT.Copy)
                    act.activation(w1_rest[u][REST:2 * REST, :], raw[0:REST, 2, :], ACT.Copy).then_inc(hi_done, 1)
                act.wait_ge(w2_in, 32)
                act.activation(w2_hi[:, :, :], raw2[:, :, :], ACT.Copy).then_inc(hi2_done, 1)
                act.activation(braw_hi[:, :], braw[:, :], ACT.Copy).then_inc(hi2_done, 1)
                act.wait_ge(rows_done, 1)
                act.activation(rows_hi[:, :, :], rps[:, :, 0:BN], ACT.Copy).then_inc(rhi_done, 1)

            @block.vector
            def _(dve):
                dve.wait_ge(hi_done, 3)
                dve.tensor_tensor(w1_lo[:, :, :], raw[:, 0:2, :], w1_hi[:, :, :], ALU.subtract)
                for u in range(2):
                    dve.tensor_tensor(w1_rest[u][2 * REST:3 * REST, :], raw[0:REST, 2, :], w1_rest[u][0:REST, :], ALU.subtract)
                dve.wait_ge(hi2_done, 2)
                dve.tensor_tensor(w2_lo[:, :, :], raw2[:, :, :], w2_hi[:, :, :], ALU.subtract)
                dve.scalar_tensor_tensor(b2[:, :], braw_hi[:, :], res["hot"][0:2, PICK:PICK + 1], braw[:, :], ALU.mult, ALU.add)
                dve.wait_ge(rhi_done, 1)
                dve.tensor_tensor(rows_lo[:, :, :], rps[:, :, 0:BN], rows_hi[:, :, :], ALU.subtract).then_inc(rlo_done, 1)

            @block.tensor
            def _(pe):
                pe.wait_ge(w_in, 64)
                for n in range(BANKS):
                    for c in range(3):
                        kk = P if c < 2 else REST + 1
                        mm = pe.matmul(rps[:, n, 0:BN], shift[0:kk, c, :], raw[0:kk, c, n * BN:(n + 1) * BN],
                                       start=(c == 0), stop=(c == 2))
                mm.then_inc(rows_done, 1)


def mlp_groups(nc, res, dram, out, l, w1, w2, b2):
    w1_hi, w1_lo, w1_rest = w1
    w2_hi, w2_lo = w2
    NG = T // GROUP
    LAG = 2
    with ExitStack() as ctx:
        k = Kit(nc, ctx, f"mg{l}_")
        xn = k.sb("xn", [P, 3 * P])
        xs = k.sb("xs", [P, 3, P])
        x_hi = [k.sb(f"x_hi{u}", [P, 2, GT], F32R) for u in range(2)]
        x_lo = [k.sb(f"x_lo{u}", [P, 2, GT], F32R) for u in range(2)]
        x_rest = [k.sb(f"x_rest{u}", [P, GT], F32R) for u in range(2)]
        hid = k.sb("hid", [P, 3, GT])
        h_hi, h_lo = k.sb("h_hi", [P, 3, GT], F32R), k.sb("h_lo", [P, 3, GT], F32R)
        ones = k.sb("ones", [2, P], F32R)
        gate = [k.sb(f"gate{u}", [P, GROUP, C]) for u in range(2)]
        upd = k.sb("upd", [P, 2, C])
        bn, mv = k.sb("bn", [P, 6]), k.sb("mv", [P, 2])
        idle_dve = k.sb("idle_dve", [P, 8])
        tp = k.ps("tp", [P, 512])
        hp = [k.ps(f"hp{i}", [P, GT]) for i in range(3)]
        yp = k.ps("yp", [P, GROUP, 512])
        s = {n: k.sem(n) for n in ("started", "init", "xn", "xT", "xs", "xhi", "xlo", "fc1", "gelu", "hhi", "hlo", "fc2", "upd", "x", "bn", "ve", "rs", "out")}
        rows_in = [k.sem(f"rows_in{u}") for u in range(2)]
        gate_in = [k.sem(f"gate_in{u}") for u in range(2)]
        scale = res[f"adapt{l}{SCALE_MLP}"]
        FIRST, EXTRA = 4, 3
        PREP = (1, 3, 5, 7)

        with nc.Block() as block:

            @block.sync
            def _(sp):
                def emit(i, u):
                    if within(i, NG):
                        wait(sp, s["fc1"], MT * (i - 1))
                        for n in range(2):
                            r = BIAS + GS * n
                            sp.dma_start(w1_rest[u][r:r + GS, :].bitcast(F32), dram[f"fc_rows{l}"][n, ds(GS * i, GS), :]).then_inc(rows_in[u], 16)
                        wait(sp, s["upd"], GROUP * (i - 1))
                        for b in range(SEQS):
                            src = dram[f"gate{l}1"][ds(GS * i, GS), :].rearrange("(j b) c -> b j c", b=SEQS)[b:b + 1]
                            sp.dma_start(gate[u][b * L:(b + 1) * L, :, :], src.broadcast_to([L, GROUP, C])).then_inc(gate_in[u], 16)
                    if l == 1 and within(i - 2, NG):
                        sp.wait_ge(s["x"], GROUP * (i - 1))
                        sp.dma_start(out[ds(GROUP * (i - 2), GROUP)].rearrange("t p c -> p t c"),
                                     res["x"][:, ds(GROUP * (i - 2), GROUP), :]).then_inc(s["out"], 16)
                steps(sp, emit, FIRST, NG, EXTRA)
                if l == 1:
                    sp.wait_ge(s["out"], 16 * NG)

            @block.gpsimd
            def _(pool):
                def prepare(i, u, j):
                    n = GROUP * i + j
                    pool.wait_ge(s["xhi"], 2 * n + 2)
                    cols = slice(j * P, (j + 1) * P)
                    pool.tensor_tensor(x_lo[u][:, :, cols], xs[:, 0:2, :], x_hi[u][:, :, cols], ALU.subtract).then_inc(s["xlo"], 1)
                    pool.wait_ge(s["xlo"], 2 * n + 1)
                    pool.tensor_tensor(x_rest[u][REST:2 * REST, cols], xs[REST:2 * REST, 2, :], x_rest[u][REST:2 * REST, cols],
                                       ALU.subtract).then_inc(s["xlo"], 1)
                    pool.wait_ge(s["xlo"], 2 * n + 2)

                def emit(i, u):
                    g = i - 2
                    if within(g, NG):
                        for j in range(GROUP):
                            n = GROUP * g + j
                            pool.wait_ge(s["upd"], n + 1)
                            pool.tensor_tensor(res["x"][:, ds(n, 1), :], res["x"][:, ds(n, 1), :], upd[:, j % 2:j % 2 + 1, :],
                                               ALU.add).then_inc(s["x"], 1)
                    for j in range(GROUP):
                        if within(i, NG):
                            prepare(i, u, j)
                        if l == 0 and within(g, NG):
                            n = GROUP * g + j
                            pool.wait_ge(s["ve"], n + 1)
                            pool.tensor_tensor(res["rs"][:, ds(n, 1)], res["ve"][:, ds(n, 1)], res["mhalf"][:, 0:1], ALU.pow)\
                                .then_inc(s["rs"], 1)
                steps(pool, emit, FIRST, NG, EXTRA)

            @block.vector
            def _(dve):
                dve.memset(idle_dve[:, :], 0.0).then_inc(s["started"], 1)
                dve.wait_ge(s["started"], 1)

                def prepare(i, u, j):
                    n = GROUP * i + j
                    normalise(dve, xn, res["x"], res["mv"], res["rs"], n).then_inc(s["xn"], 1)
                    dve.wait_ge(s["xT"], n + 1)
                    wait(dve, s["xlo"], 2 * n)
                    b = scale[:, :, ds(SEQS * n, SEQS)].unsqueeze(3).broadcast_to([P, 3, SEQS, L])
                    dve.tensor_tensor(xs[:, :, :].rearrange("p c (b q) -> p c b q", b=SEQS),
                                      tp[:, 0:3 * P].rearrange("p (c b q) -> p c b q", c=3, b=SEQS), b, ALU.mult).then_inc(s["xs"], 1)

                def emit(i, u):
                    g = i - 2
                    if within(g, NG):
                        dve.wait_ge(gate_in[u], parity_count(g, u, 32))
                        dve.wait_ge(s["fc2"], MT * (g + 1))
                        for j in range(GROUP):
                            n = GROUP * g + j
                            wait(dve, s["x"], n - 1)
                            dve.tensor_tensor(upd[:, j % 2, :], yp[:, j, 0:C], gate[u][:, j, :], ALU.mult).then_inc(s["upd"], 1)
                    g = i - 1
                    for m in range(MT):
                        if within(g, NG):
                            dve.wait_ge(s["gelu"], MT * g + m + 1)
                            wait(dve, s["fc2"], MT * g + m - 2)
                            dve.tensor_copy(h_hi[:, m % 3, :], hid[:, m % 3, :]).then_inc(s["hhi"], 1)
                            dve.wait_ge(s["hhi"], MT * g + m + 1)
                            dve.tensor_tensor(h_lo[:, m % 3, :], hid[:, m % 3, :], h_hi[:, m % 3, :], ALU.subtract).then_inc(s["hlo"], 1)
                        if within(i, NG) and m in PREP:
                            prepare(i, u, PREP.index(m))
                        if l == 0 and within(i - 2, NG) and m in PREP:
                            n = GROUP * (i - 2) + PREP.index(m)
                            dve.wait_ge(s["x"], n + 1)
                            dve.bn_stats(bn[:, :], res["x"][:, ds(n, 1), :]).then_inc(s["bn"], 1)
                            wait_apart(dve, idle_dve, 4, s["bn"], 2 * n + 1)
                            dve.bn_aggr(mv[:, :], bn[:, :]).then_inc(s["bn"], 1)
                            dve.wait_ge(s["bn"], 2 * n + 2)
                            dve.tensor_copy(res["mv"][:, ds(n, 1), 0], mv[:, 0:1])
                            dve.tensor_scalar(res["ve"][:, ds(n, 1)], mv[:, 1:2], EPS, None, ALU.add).then_inc(s["ve"], 1)
                steps(dve, emit, FIRST, NG, EXTRA)

            @block.scalar
            def _(act):
                for u in range(2):
                    act.activation(x_rest[u][BIAS:BIAS + 2 * GS, :], res["hot"][BIAS:BIAS + 2 * GS, P:P + GT], ACT.Copy)
                act.activation(ones[:, :], res["hot"][0:2, ONES:], ACT.Copy).then_inc(s["init"], 1)

                def prepare(i, u, j):
                    n = GROUP * i + j
                    cols = slice(j * P, (j + 1) * P)
                    act.wait_ge(s["xs"], n + 1)
                    if j == 0:
                        wait(act, s["fc1"], MT * (i - 1))
                    act.activation(x_hi[u][:, :, cols], xs[:, 0:2, :], ACT.Copy).then_inc(s["xhi"], 1)
                    act.activation(x_rest[u][0:BIAS, cols], xs[0:BIAS, 2, :], ACT.Copy).then_inc(s["xhi"], 1)

                def emit(i, u):
                    g = i - 1
                    for m in range(MT):
                        if within(g, NG):
                            act.wait_ge(s["fc1"], MT * g + m + 1)
                            wait(act, s["hlo"], MT * g + m - 2)
                            act.activation(hid[:, m % 3, :], hp[m % 3][:, :], ACT.Gelu_apprx_tanh).then_inc(s["gelu"], 1)
                        if within(i, NG) and m in PREP:
                            prepare(i, u, PREP.index(m))
                steps(act, emit, FIRST, NG, EXTRA)

            @block.tensor
            def _(pe):
                pe.wait_ge(s["init"], 1)

                def fc1(g, u, m):
                    wait(pe, s["gelu"], MT * g + m - 2)
                    cols = slice(m * P, (m + 1) * P)
                    dst, rest = hp[m % 3][:, :], BIAS + 2 * GS
                    pe.matmul(dst, w1_rest[u][0:rest, cols], x_rest[u][0:rest, :], start=True, stop=False)
                    for c in range(2):
                        pe.matmul(dst, w1_hi[:, c, cols], x_hi[u][:, c, :], start=False, stop=False)
                        pe.matmul(dst, w1_hi[:, c, cols], x_lo[u][:, c, :], start=False, stop=False)
                        last = pe.matmul(dst, w1_lo[:, c, cols], x_hi[u][:, c, :], start=False, stop=(c == 1))
                    last.then_inc(s["fc1"], 1)

                def fc2(g, m):
                    pe.wait_ge(s["hlo"], MT * g + m + 1)
                    if m == 0:
                        wait(pe, s["upd"], GROUP * g)
                    for j in range(GROUP):
                        cols, dst, r = slice(j * P, (j + 1) * P), yp[:, j, 0:C], m % 3
                        if m == 0:
                            pe.matmul(dst, ones[:, :], b2[:, :], start=True, stop=False)
                        pe.matmul(dst, h_hi[:, r, cols], w2_hi[:, m, :], start=False, stop=False)
                        pe.matmul(dst, h_hi[:, r, cols], w2_lo[:, m, :], start=False, stop=False)
                        last = pe.matmul(dst, h_lo[:, r, cols], w2_hi[:, m, :], start=False, stop=(m == MT - 1))
                    last.then_inc(s["fc2"], 1)

                def emit(i, u):
                    g = i - 1
                    if within(g, NG):
                        pe.wait_ge(s["xhi"], 2 * GROUP * (g + 1))
                        pe.wait_ge(s["xlo"], 2 * GROUP * (g + 1))
                        pe.wait_ge(rows_in[1 - u], parity_count(g, 1 - u, 32))
                    for m in range(MT + LAG):
                        if within(g, NG):
                            if m < MT:
                                fc1(g, 1 - u, m)
                            if m >= LAG:
                                fc2(g, m - LAG)
                        if within(i, NG) and m in PREP:
                            n = GROUP * i + PREP.index(m)
                            pe.wait_ge(s["xn"], n + 1)
                            wait(pe, s["xs"], n)
                            transposes(pe, tp, xn, xn[:, 2 * P:3 * P], res["ident"]).then_inc(s["xT"], 1)
                steps(pe, emit, FIRST, NG, EXTRA)


def program(nc, w, out):
    with ExitStack() as ctx:
        k = Kit(nc, ctx, "")
        res = {
            "x": k.sb("x", [P, T, C]),
            "ident": k.sb("ident", [P, P]), "ident_r": k.sb("ident_r", [P, P], F32R),
            "hot": k.sb("hot", [P, ONES + P]),
            "mv": k.sb("mv", [P, T, 2]), "ve": k.sb("ve", [P, T]), "rs": k.sb("rs", [P, T]), "mhalf": k.sb("mhalf", [P, T]),
        }
        dram = {}
        for l in range(2):
            for part in (SHIFT_MSA, SCALE_MSA, SHIFT_MLP, SCALE_MLP):
                res[f"adapt{l}{part}"] = k.sb(f"adapt{l}{part}", [P, 3, P])
            dram[f"qkv_rows{l}"] = nc.dram_tensor(f"qkv_rows{l}", (2, B, 2 * QKVH), F32, kind="Internal").ap()
            dram[f"fc_rows{l}"] = nc.dram_tensor(f"fc_rows{l}", (2, B, FF), F32, kind="Internal").ap()
            for g in range(2):
                dram[f"gate{l}{g}"] = nc.dram_tensor(f"gate{l}{g}", (B, C), F32, kind="Internal").ap()
        modulation(nc, w, res, dram)
        for l in range(2):
            attention(nc, w, res, dram, l)
            mlp(nc, w, res, dram, out, l)


def constants():
    import numpy as np
    hot = np.zeros((2 * GS, ONES + P), np.float32)
    for r in range(2 * GS):
        if r < 2 * SEQS:
            hot[r, 0:P] = np.arange(P) // L == r % SEQS
        hot[r, P:P + GT] = np.arange(GT) // L == r % GS
    hot[1, PICK] = -1.0
    hot[:, ONES:] = 1.0
    return hot, np.eye(P, dtype=np.float32)


NAMES = {"x": "x", "cond_1152": "cond_1152", "gain0": "L0_cond_g_q", "gain1": "L0_cond_g_k"}
for _l, _names in enumerate((
        dict(mod="w_mod b_mod", qkv="w_qkv b_qkv", o="w_proj b_proj", fc1="w1 b1", fc2="w2 b2"),
        dict(mod="W_ada b_ada", qkv="W_qkv b_qkv", o="W_proj b_proj", fc1="W_fc1 b_fc1", fc2="W_fc2 b_fc2"))):
    for _k, _v in _names.items():
        for _kind, _n in zip("wb", _v.split()):
            NAMES[f"{_k}_{_kind}{_l}"] = f"L{_l}_cond_{_n}"


def kernel(**inputs):
    import numpy as np
    import concourse.bacc as bacc
    from concourse.bass_utils import run_bass_kernel_spmd

    nc = bacc.Bacc("TRN2", target_bir_lowering=False, num_devices=1)
    hot, ident = constants()
    arrays = {"hot": hot, "ident": ident}
    for name, theirs in NAMES.items():
        a = np.ascontiguousarray(inputs[theirs])
        if name == "x":
            a = a.reshape(T, P, C)
        if a.ndim == 1:
            a = a.reshape(1, -1)
        arrays[name] = a
    w = {n: nc.dram_tensor(f"in_{n}", a.shape, mybir.dt.from_np(a.dtype), kind="ExternalInput").ap() for n, a in arrays.items()}
    out = nc.dram_tensor("out_x", (T, P, C), F32, kind="ExternalOutput").ap()
    program(nc, w, out)
    r = run_bass_kernel_spmd(nc, [{f"in_{n}": a for n, a in arrays.items()}], core_ids=[0])
    return r.results[0]["out_x"].reshape(B, L, C)
```

```python
from contextlib import ExitStack

import concourse.bass as bass
from concourse import mybir

ACT = mybir.ActivationFunctionType
ALU = mybir.AluOpType
AX = mybir.AxisListType
F32 = mybir.dt.float32
F32R = mybir.dt.float32r
I32 = mybir.dt.int32
ds = bass.ds

P = 128
B, L, C = 128, 64, 288
NH, HD = 16, 18
FF = 4 * C
T = B * L // P
SEQS = P // L
EPS = 1e-6
REST = C - 2 * P
BIAS = 3 * REST
SLOT = 64
PAIRS = NH // 2
HALF = NH // 2 * HD
QKVH = 3 * HALF
VW = HD + 1
GROUP = 4
TURN = 4
GT = GROUP * P
GS = GROUP * SEQS
MT = FF // P
GUESS = float(0x5F3759DF - (1 << 22) - (1 << 30))
PICK, ONES = P + GT, P + GT + 1
SHIFT_MSA, SCALE_MSA, GATE_MSA, SHIFT_MLP, SCALE_MLP, GATE_MLP = range(6)


def wait(eng, sem, value):
    if not isinstance(value, int) or value > 0:
        eng.wait_ge(sem, value)


def steps(eng, emit, first, last, extra, turn=2):
    for i in range(first):
        emit(i, i % turn)
    with eng.Fori(first // turn, last // turn) as r:
        for u in range(turn):
            emit(turn * r + u, u)
    for i in range(last, last + extra):
        emit(i, i % turn)


def wait_apart(eng, idle, column, sem, value):
    eng.wait_ge(sem, value)
    eng.tensor_tensor(idle[:, column:column + 1], idle[:, 0:1], idle[:, 0:1], ALU.mult)


def within(t, n):
    return not isinstance(t, int) or 0 <= t < n


class Kit:

    def __init__(self, nc, ctx, prefix):
        self.nc, self.ctx, self.prefix, self.sems = nc, ctx, prefix, []
        ctx.callback(self.clear)

    def sb(self, name, shape, dt=F32):
        return self.ctx.enter_context(self.nc.sbuf_tensor(self.prefix + name, shape, dt))

    def ps(self, name, shape):
        return self.ctx.enter_context(self.nc.psum_tensor(self.prefix + name, shape, F32))

    def sem(self, name):
        made = self.nc.alloc_semaphore(self.prefix + name)
        self.sems.append(made)
        return made

    def clear(self):
        if self.sems:
            self.nc.clear_and_free_semaphores(self.sems)
            self.nc.all_engine_barrier()


def upto(t):
    return min(t + 1, T) if isinstance(t, int) else t + 1


def parity_count(t, parity, each):
    return each // 2 * (t - parity) + each


def three(pe, dst, cols, acts, weights, rest_rows):
    (a_hi, a_lo, a_rest), (w_hi, w_lo, w_rest) = acts, weights
    pe.matmul(dst, a_rest[0:rest_rows, :], w_rest[0:rest_rows, cols], start=True, stop=False)
    for c in range(2):
        pe.matmul(dst, a_hi[:, c, :], w_hi[:, c, cols], start=False, stop=False)
        pe.matmul(dst, a_hi[:, c, :], w_lo[:, c, cols], start=False, stop=False)
        last = pe.matmul(dst, a_lo[:, c, :], w_hi[:, c, cols], start=False, stop=(c == 1))
    return last


def transposes(pe, out, tile, rest, ident):
    pe.transpose(out[:, 0:P], tile[:, 0:P], ident[:, :])
    pe.transpose(out[:, P:2 * P], tile[:, P:2 * P], ident[:, :])
    return pe.transpose(out[:, 2 * P:3 * P], rest, ident[:, :])


def normalise(act, xn, res, t):
    nb, rs, x = res["nb"][:, ds(t, 1)], res["rs"][:, ds(t, 1)], res["x"]
    act.activation(xn[:, 0:2 * P].unsqueeze(1), x[:, ds(t, 1), 0:2 * P], ACT.Identity, bias=nb, scale=rs)
    return act.activation(xn[:, 2 * P:3 * P].rearrange("p (a r) -> p a r", a=4), x[:, ds(t, 1), 2 * P:C].broadcast_to([P, 4, REST]),
                          ACT.Identity, bias=nb, scale=rs)


def statistics(dve, res, s, bn, mv, idle, column, t):
    dve.wait_ge(s["x"], t + 1)
    dve.bn_stats(bn[:, :], res["x"][:, ds(t, 1), :]).then_inc(s["bn"], 1)
    wait_apart(dve, idle, column, s["bn"], 2 * t + 1)
    dve.bn_aggr(mv[:, :], bn[:, :]).then_inc(s["bn"], 1)
    dve.wait_ge(s["bn"], 2 * t + 2)
    dve.tensor_scalar(res["nm"][:, ds(t, 1)], mv[:, 0:1], -1.0, None, ALU.mult)
    dve.tensor_scalar(res["ve"][:, ds(t, 1)], mv[:, 1:2], EPS, None, ALU.add).then_inc(s["ve"], 1)


def factors(pool, res, s, t):
    pool.wait_ge(s["ve"], t + 1)
    pool.tensor_tensor(res["rs"][:, ds(t, 1)], res["ve"][:, ds(t, 1)], res["mhalf"][:, 0:1], ALU.pow).then_inc(s["rs"], 1)
    pool.wait_ge(s["rs"], 2 * t + 1)
    pool.tensor_tensor(res["nb"][:, ds(t, 1)], res["nm"][:, ds(t, 1)], res["rs"][:, ds(t, 1)], ALU.mult).then_inc(s["rs"], 1)


def modulation(nc, w, res, dram):
    with ExitStack() as ctx:
        k = Kit(nc, ctx, "mod_")
        cond = k.sb("cond", [P, C])
        ex = k.sb("ex", [P, C])
        den = k.sb("den", [P, C])
        rec = k.sb("rec", [P, C])
        silu = k.sb("silu", [P, C])
        condT = k.sb("condT", [P, 3, P])
        wm = k.sb("wm", [P, 3, 6 * C])
        wm_rest = k.sb("wm_rest", [P, 3, 4, P])
        gates = k.sb("gates", [P, 2, C])
        bn, mv = k.sb("bn", [P, 2, 6]), k.sb("mv", [P, T, 2])
        tr = k.ps("tr", [P, 3, P])
        feat = [k.ps(f"feat{i}", [P, 3, P]) for i in range(2)]
        gps = [k.ps(f"gps{i}", [P, C]) for i in range(2)]
        cond_in, x_in, ident_in = k.sem("cond_in"), [k.sem(f"x_in{i}") for i in range(8)], k.sem("ident_in")
        w_in = [k.sem(f"w_in{i}") for i in range(2)]
        exp_done, add_done, rec_done, silu_done = k.sem("exp"), k.sem("add"), k.sem("rec"), k.sem("silu")
        tr_done, condT_done = k.sem("tr_done"), k.sem("condT_done")
        feat_done, feat_read = k.sem("feat_done"), k.sem("feat_read")
        gate_done, gate_read, gate_out = k.sem("gate_done"), k.sem("gate_read"), k.sem("gate_out")
        bn_done, var_done, ones_done = k.sem("bn_done"), k.sem("var_done"), k.sem("ones_done")
        oh_in, rs_done, dup_done = k.sem("oh_in"), k.sem("rs_done"), k.sem("dup_done")
        ADAPT = [(SCALE_MSA, 1.0), (SHIFT_MSA, 0.0), (SCALE_MLP, 1.0), (SHIFT_MLP, 0.0)]

        with nc.Block() as block:

            @block.sync
            def _(sp):
                sp.dma_start(cond[:, :], w["cond_1152"]).then_inc(cond_in, 16)
                sp.dma_start(res["ident"][:, :], w["ident"]).then_inc(ident_in, 16)
                for l in range(2):
                    if l:
                        sp.wait_ge(feat_done, 4)
                        sp.wait_ge(gate_done, 2)
                    wmod, bmod = w[f"mod_w{l}"], w[f"mod_b{l}"]
                    for c in range(2):
                        sp.dma_start(wm[:, c, :], wmod[c * P:(c + 1) * P, :]).then_inc(w_in[l], 16)
                    sp.dma_start(wm[0:REST, 2, :], wmod[2 * P:C, :]).then_inc(w_in[l], 16)
                    sp.dma_start(wm[REST:REST + 1, 2, :], bmod).then_inc(w_in[l], 16)
                    if not l:
                        for n in range(8):
                            sp.dma_start(res["x"][:, 8 * n:8 * n + 8, :],
                                         w["x"][8 * n:8 * n + 8].rearrange("t p c -> p t c")).then_inc(x_in[n], 16)
                        sp.dma_start(res["hot"][BIAS:BIAS + 2 * GS, :], w["hot"]).then_inc(oh_in, 16)
                        sp.dma_start(res["hot"][0:2, :], w["hot"][0:2, :]).then_inc(oh_in, 16)
                sp.wait_ge(oh_in, 32)

            @block.scalar
            def _(act):
                act.wait_ge(ident_in, 16)
                act.activation(res["ident_r"][:, :], res["ident"][:, :], ACT.Copy)
                act.wait_ge(cond_in, 16)
                act.activation(ex[:, :], cond[:, :], ACT.Exp, scale=-1.0).then_inc(exp_done, 1)
                act.wait_ge(tr_done, 3)
                act.activation(condT[:, 0:2, :], tr[:, 0:2, :], ACT.Copy).then_inc(condT_done, 1)
                act.activation(condT[0:REST, 2, :], tr[0:REST, 2, :], ACT.Copy).then_inc(condT_done, 1)
                for l in range(2):
                    for g in range(2):
                        act.wait_ge(gate_done, 2 * l + g + 1)
                        if l:
                            act.wait_ge(gate_out, 32)
                        act.activation(gates[:, g, :], gps[g][:, :], ACT.Copy).then_inc(gate_read, 1)
                    for g in range(2):
                        act.wait_ge(gate_read, 2 * l + g + 1)
                        act.dma_start(dram[f"gate{l}{g}"], gates[:, g, :]).then_inc(gate_out, 16)
                act.wait_ge(gate_out, 64)

            @block.tensor
            def _(pe):
                pe.wait_ge(ident_in, 16)
                pe.wait_ge(silu_done, 1)
                for c in range(3):
                    n = P if c < 2 else REST
                    pe.transpose(tr[0:n, c, :], silu[:, c * P:c * P + n], res["ident"][:, :]).then_inc(tr_done, 1)
                pe.wait_ge(condT_done, 2)
                pe.wait_ge(ones_done, 1)
                for l in range(2):
                    pe.wait_ge(w_in[l], 64)
                    for g, part in enumerate((GATE_MSA, GATE_MLP)):
                        wait(pe, gate_read, 2 * (l - 1) + g + 1)
                        for c in range(3):
                            n = P if c < 2 else REST + 1
                            mm = pe.matmul(gps[g][:, :], condT[0:n, c, :], wm[0:n, c, part * C:(part + 1) * C],
                                           start=(c == 0), stop=(c == 2))
                        mm.then_inc(gate_done, 1)
                    pe.wait_ge(dup_done, l + 1)
                    for j, (part, _) in enumerate(ADAPT):
                        m = 4 * l + j
                        wait(pe, feat_read, m - 1)
                        for o in range(3):
                            for c in range(3):
                                n = P if c < 2 else REST + 1
                                cols = wm[0:n, c, part * C + o * P:part * C + (o + 1) * P] if o < 2 else wm_rest[0:n, c, j, :]
                                mm = pe.matmul(feat[m % 2][:, o, :], cols, condT[0:n, c, :],
                                               start=(c == 0), stop=(c == 2))
                        mm.then_inc(feat_done, 1)

            @block.vector
            def _(dve):
                dve.memset(condT[REST:REST + 1, 2, :], 1.0).then_inc(ones_done, 1)
                dve.wait_ge(exp_done, 1)
                dve.tensor_scalar(den[:, :], ex[:, :], 1.0, None, ALU.add).then_inc(add_done, 1)
                dve.wait_ge(add_done, 1)
                dve.reciprocal(rec[:, :], den[:, :]).then_inc(rec_done, 1)
                dve.wait_ge(rec_done, 1)
                dve.tensor_tensor(silu[:, :], cond[:, :], rec[:, :], ALU.mult).then_inc(silu_done, 1)
                for l in range(2):
                    for j, (part, plus) in enumerate(ADAPT):
                        m = 4 * l + j
                        dve.wait_ge(feat_done, m + 1)
                        dst = res[f"adapt{l}{part}"]
                        dve.tensor_scalar(dst[:, :, :], feat[m % 2][:, :, :], plus, None, ALU.add).then_inc(feat_read, 1)
                        if part in (SHIFT_MSA, SHIFT_MLP):
                            dve.wait_ge(feat_read, m + 1)
                            dve.memset(dst[REST:REST + 1, 2, :], 1.0)
                for t in range(T):
                    if t % 8 == 0:
                        dve.wait_ge(x_in[t // 8], 16)
                    wait(dve, bn_done, 2 * (t - 1))
                    dve.bn_stats(bn[:, t % 2, :], res["x"][:, t, :]).then_inc(bn_done, 1)
                    dve.wait_ge(bn_done, 2 * t + 1)
                    dve.bn_aggr(mv[:, t, :], bn[:, t % 2, :]).then_inc(bn_done, 1)
                dve.wait_ge(bn_done, 2 * T)
                dve.tensor_scalar(res["nm"][:, :], mv[:, :, 0], -1.0, None, ALU.mult)
                dve.tensor_scalar(res["ve"][:, :], mv[:, :, 1], EPS, None, ALU.add).then_inc(var_done, 1)

            @block.gpsimd
            def _(pool):
                pool.memset(res["mhalf"][:, :], -0.5).then_inc(rs_done, 1)
                for l in range(2):
                    pool.wait_ge(w_in[l], 64)
                    if l:
                        pool.wait_ge(feat_done, 4)
                    for j, (part, _) in enumerate(ADAPT):
                        for n, c in ((P, slice(0, 2)), (REST + 1, slice(2, 3))):
                            src = wm[0:n, c, part * C + 2 * P:(part + 1) * C]
                            last = pool.tensor_copy(wm_rest[0:n, c, j, :].rearrange("p c (a r) -> p c a r", a=4),
                                                    src.unsqueeze(2).broadcast_to([n, src.shape[1], 4, REST]))
                    last.then_inc(dup_done, 1)
                pool.wait_ge(rs_done, 1)
                pool.wait_ge(var_done, 1)
                pool.tensor_tensor(res["rs"][:, :], res["ve"][:, :], res["mhalf"][:, :], ALU.pow).then_inc(rs_done, 1)
                pool.wait_ge(rs_done, 2)
                pool.tensor_tensor(res["nb"][:, :], res["nm"][:, :], res["rs"][:, :], ALU.mult)


def attention(nc, w, res, dram, l):
    with ExitStack() as ctx:
        k = Kit(nc, ctx, f"att{l}_")
        wqkv_hi, wqkv_lo = k.sb("wqkv_hi", [P, 2, 2 * QKVH], F32R), k.sb("wqkv_lo", [P, 2, 2 * QKVH], F32R)
        wqkv_rest = [k.sb(f"wqkv_rest{u}", [P, 2 * QKVH], F32R) for u in range(2)]
        wo_hi, wo_lo, wo_rest = k.sb("wo_hi", [P, 2, C], F32R), k.sb("wo_lo", [P, 2, C], F32R), k.sb("wo_rest", [P, C], F32R)
        gains = k.sb("gains", [P, HD])
        attention_weights(nc, w, res, dram, l, wqkv_hi, wqkv_lo, wqkv_rest, wo_hi, wo_lo, wo_rest, gains)
        attention_tiles(nc, w, res, dram, l, wqkv_hi, wqkv_lo, wqkv_rest, wo_hi, wo_lo, wo_rest, gains)


def attention_weights(nc, w, res, dram, l, wqkv_hi, wqkv_lo, wqkv_rest, wo_hi, wo_lo, wo_rest, gains):
    with ExitStack() as ctx:
        k = Kit(nc, ctx, f"aw{l}_")
        raw = k.sb("raw", [P, 3, 2 * QKVH])
        oraw = k.sb("oraw", [P, 3, C])
        obias, obias_hi = k.sb("obias", [P, C]), k.sb("obias_hi", [P, C], F32R)
        means = k.sb("means", [P, 3, 4 * 8])
        rows_hi, rows_lo = k.sb("rows_hi", [P, 2, QKVH], F32R), k.sb("rows_lo", [P, 2, QKVH], F32R)
        gq = k.sb("gq", [P, 2, HD])
        rps = k.ps("rps", [P, 2, 512])
        w_in, o_in, g_in = k.sem("w_in"), k.sem("o_in"), k.sem("g_in")
        mean_done, ready = k.sem("mean_done"), k.sem("ready")
        hi_done, lo_done, ohi_done, rows_done, rhi_done, rlo_done, rows_out = (
            k.sem(n) for n in ("hi", "lo", "ohi", "rows", "rhi", "rlo", "rows_out"))
        shift = res[f"adapt{l}{SHIFT_MSA}"]
        BLOCKS = [(P, slice(0, 2)), (REST + 1, slice(2, 3))]
        with nc.Block() as block:

            @block.sync
            def _(sp):
                wq, bq = w[f"qkv_w{l}"], w[f"qkv_b{l}"]
                for n in range(2):
                    for s in range(3):
                        src = slice(s * C + n * HALF, s * C + (n + 1) * HALF)
                        dst = slice(n * QKVH + s * HALF, n * QKVH + (s + 1) * HALF)
                        sp.dma_start(raw[:, 0:2, dst], wq[0:2 * P, src].rearrange("(c p) n -> p c n", c=2)).then_inc(w_in, 16)
                        sp.dma_start(raw[0:REST, 2, dst], wq[2 * P:C, src]).then_inc(w_in, 16)
                        sp.dma_start(raw[REST:REST + 1, 2, dst], bq[:, src]).then_inc(w_in, 16)
                wo, bo = w[f"o_w{l}"], w[f"o_b{l}"]
                sp.dma_start(oraw[:, 0:2, :], wo[0:2 * P, :].rearrange("(c p) n -> p c n", c=2)).then_inc(o_in, 16)
                sp.dma_start(oraw[0:REST, 2, :], wo[2 * P:C, :]).then_inc(o_in, 16)
                sp.dma_start(obias[BIAS:BIAS + 2, :], bo.broadcast_to([2, C])).then_inc(o_in, 16)
                if l == 0:
                    for s in range(2):
                        sp.dma_start(gq[:, s, :], w[f"gain{s}"].broadcast_to([P, HD])).then_inc(g_in, 16)
                for n, (done, rows) in enumerate(((rhi_done, rows_hi), (rlo_done, rows_lo))):
                    sp.wait_ge(done, 1)
                    sp.dma_start(dram[f"qkv_rows{l}"][n], rows[:, :, :].rearrange("p a b -> p (a b)").bitcast(F32)).then_inc(rows_out, 16)
                sp.wait_ge(rows_out, 32)

            @block.vector
            def _(dve):
                dve.wait_ge(w_in, 9 * 2 * 16)
                if l == 0:
                    for i, (rows, c) in enumerate(BLOCKS):
                        nchunk = c.stop - c.start
                        heads = [raw[0:rows, c, n * QKVH:n * QKVH + 2 * HALF].rearrange("p c (h d) -> p c h d", d=HD) for n in range(2)]
                        for n in range(2):
                            mean = means[0:rows, c, 16 * n:16 * n + 16]
                            dve.tensor_reduce(mean, heads[n], AX.X, ALU.add).then_inc(mean_done, 1)
                            dve.wait_ge(mean_done, 3 * (2 * i + n) + 1)
                            dve.tensor_scalar(mean, mean, 1.0 / HD, None, ALU.mult).then_inc(mean_done, 1)
                            dve.wait_ge(mean_done, 3 * (2 * i + n) + 2)
                            for cc in range(nchunk):
                                last = dve.tensor_tensor(heads[n][:, cc], heads[n][:, cc],
                                                         mean[:, cc].unsqueeze(2).broadcast_to([rows, 16, HD]), ALU.subtract)
                            last.then_inc(mean_done, 1)
                    dve.wait_ge(g_in, 32)
                    dve.tensor_scalar(gq[:, 0, :], gq[:, 0, :], float(HD) ** -0.5, None, ALU.mult).then_inc(mean_done, 1)
                    dve.wait_ge(mean_done, 13)
                    dve.tensor_tensor(gains[:, :], gq[:, 0, :], gq[:, 1, :], ALU.mult).then_inc(ready, 1)
                else:
                    for rows, c in BLOCKS:
                        for n in range(2):
                            kcols = raw[0:rows, c, n * QKVH + HALF:n * QKVH + 2 * HALF]
                            last = dve.tensor_scalar(kcols, kcols, float(HD) ** -0.5, None, ALU.mult)
                    last.then_inc(ready, 1)
                dve.wait_ge(hi_done, 3)
                dve.tensor_tensor(wqkv_lo[:, :, :], raw[:, 0:2, :], wqkv_hi[:, :, :], ALU.subtract).then_inc(lo_done, 1)
                for u in range(2):
                    dve.tensor_tensor(wqkv_rest[u][2 * REST:3 * REST, :], raw[0:REST, 2, :], wqkv_rest[u][0:REST, :],
                                      ALU.subtract).then_inc(lo_done, 1)
                dve.wait_ge(ohi_done, 4)
                dve.tensor_tensor(wo_lo[:, :, :], oraw[:, 0:2, :], wo_hi[:, :, :], ALU.subtract).then_inc(lo_done, 1)
                dve.tensor_tensor(wo_rest[2 * REST:3 * REST, :], oraw[0:REST, 2, :], wo_rest[0:REST, :], ALU.subtract).then_inc(lo_done, 1)
                dve.scalar_tensor_tensor(wo_rest[BIAS:BIAS + 2, :], obias_hi[BIAS:BIAS + 2, :], res["hot"][BIAS:BIAS + 2, PICK:PICK + 1],
                                         obias[BIAS:BIAS + 2, :], ALU.mult, ALU.add).then_inc(lo_done, 1)
                dve.wait_ge(rhi_done, 1)
                dve.tensor_tensor(rows_lo[:, :, :], rps[:, :, 0:QKVH], rows_hi[:, :, :], ALU.subtract).then_inc(rlo_done, 1)

            @block.scalar
            def _(act):
                act.wait_ge(o_in, 48)
                act.activation(wo_hi[:, :, :], oraw[:, 0:2, :], ACT.Copy).then_inc(ohi_done, 1)
                act.activation(wo_rest[0:REST, :], oraw[0:REST, 2, :], ACT.Copy).then_inc(ohi_done, 1)
                act.activation(wo_rest[REST:2 * REST, :], oraw[0:REST, 2, :], ACT.Copy).then_inc(ohi_done, 1)
                act.activation(obias_hi[BIAS:BIAS + 2, :], obias[BIAS:BIAS + 2, :], ACT.Copy).then_inc(ohi_done, 1)
                act.wait_ge(ready, 1)
                act.activation(wqkv_hi[:, :, :], raw[:, 0:2, :], ACT.Copy).then_inc(hi_done, 1)
                for u in range(2):
                    act.activation(wqkv_rest[u][0:REST, :], raw[0:REST, 2, :], ACT.Copy)
                    act.activation(wqkv_rest[u][REST:2 * REST, :], raw[0:REST, 2, :], ACT.Copy).then_inc(hi_done, 1)
                act.wait_ge(rows_done, 1)
                act.activation(rows_hi[:, :, :], rps[:, :, 0:QKVH], ACT.Copy).then_inc(rhi_done, 1)

            @block.tensor
            def _(pe):
                pe.wait_ge(ready, 1)
                for n in range(2):
                    for c in range(3):
                        kk = P if c < 2 else REST + 1
                        mm = pe.matmul(rps[:, n, 0:QKVH], shift[0:kk, c, :], raw[0:kk, c, n * QKVH:(n + 1) * QKVH],
                                       start=(c == 0), stop=(c == 2))
                mm.then_inc(rows_done, 1)


XT_BANK, QT_BANK, KT_BANK, OT_BANK, PT_BANK = 1, (0, 1), (0, 1), 0, (1, 0)


def attention_tiles(nc, w, res, dram, l, wqkv_hi, wqkv_lo, wqkv_rest, wo_hi, wo_lo, wo_rest, gains):
    with ExitStack() as ctx:
        k = Kit(nc, ctx, f"at{l}_")
        normed = l == 0
        xn = k.sb("xn", [P, 3 * P])
        xs = k.sb("xs", [P, 3, P])
        x_hi, x_lo, x_rest = k.sb("x_hi", [P, 2, P], F32R), k.sb("x_lo", [P, 2, P], F32R), k.sb("x_rest", [P, P], F32R)
        qk = k.sb("qk", [P, 2, 2, 8, HD])
        sq = k.sb("sq", [P, 2, 16 * HD])
        ss, vh, y0, t0, t1, three_halves = (k.sb(n, [P, 32]) for n in ("ss", "vh", "y0", "t0", "t1", "three_halves"))
        stack = [k.sb(f"stack{u}", [P, 2, 2, 8, SLOT], F32R) for u in range(2)]
        vals = [k.sb(f"vals{u}", [P, SEQS, NH, VW]) for u in range(TURN)]
        qT = k.sb("qT", [P, PAIRS, SEQS, 2, L], F32R)
        kT = k.sb("kT", [P, PAIRS, SEQS, L], F32R)
        mx = k.sb("mx", [P, 16])
        sd = k.sb("sd", [P, 16, L])
        pr = k.sb("pr", [P, 16, L])
        prT = k.sb("prT", [P, PAIRS, P])
        rc = k.sb("rc", [P, 2, 16])
        idle_pool, idle_dve = k.sb("idle_pool", [P, 8]), k.sb("idle_dve", [P, 8])
        o = [k.sb(f"o{u}", [P, NH, HD]) for u in range(2)]
        o_dup = [k.sb(f"o_dup{u}", [P, P]) for u in range(2)]
        o_hi, o_lo, o_rest = k.sb("o_hi", [P, 2, P], F32R), k.sb("o_lo", [P, 2, P], F32R), k.sb("o_rest", [P, P], F32R)
        gate = [k.sb(f"gate{u}", [P, C]) for u in range(2)]
        upd = k.sb("upd", [P, 2, C])
        bn, mv = k.sb("bn", [P, 6]), k.sb("mv", [P, 2])
        tp, qp, sp_, op = (k.ps(n, [P, 2, 512]) for n in ("tp", "qp", "sp", "op"))
        s = {n: k.sem(n) for n in (
            "started", "zero", "init", "xn", "xT", "xs", "xhi", "xlo", "qkv", "sq", "ss", "vh", "rr", "gk", "qraw", "qn", "kn", "khi", "vals",
            "klo", "kdup", "qTt", "kTt", "qTa", "qTd", "kTa", "score", "mx", "sub", "exp", "prT", "prTe", "pv", "rc", "o",
            "odup", "oT", "ohi", "olo", "proj", "upd", "x", "bn", "ve", "rs", "nw")}
        rows_in = [k.sem(f"rows_in{u}") for u in range(2)]
        gate_in = [k.sem(f"gate_in{u}") for u in range(2)]
        FIRST, LAST, EXTRA = 8, T - TURN, 8
        scale = res[f"adapt{l}{SCALE_MSA}"]

        with nc.Block() as block:

            @block.sync
            def _(sp):
                def emit(i, u):
                    t, v = i, u % 2
                    if within(t, T):
                        wait(sp, s["qkv"], t - 1)
                        for n in range(2):
                            r = BIAS + SEQS * n
                            sp.dma_start(wqkv_rest[v][r:r + SEQS, :].bitcast(F32),
                                         dram[f"qkv_rows{l}"][n, ds(SEQS * t, SEQS), :]).then_inc(rows_in[v], 16)
                    t = i - 4
                    if within(t, T):
                        wait(sp, s["upd"], t - 1)
                        for b in range(SEQS):
                            sp.dma_start(gate[v][b * L:(b + 1) * L, :],
                                         dram[f"gate{l}0"][ds(SEQS * t + b, 1), :].broadcast_to([L, C])).then_inc(gate_in[v], 16)
                steps(sp, emit, FIRST, LAST, T - LAST + 4, TURN)

            @block.gpsimd
            def _(pool):
                for u in range(2):
                    pool.memset(stack[u][:, :, :, :, 3 * HD:SLOT].bitcast(F32), 0.0).then_inc(s["init"], 1)
                pool.memset(qT[:, :, :, :, :].bitcast(F32), 0.0).then_inc(s["init"], 1)
                pool.memset(idle_pool[:, :], 0.0).then_inc(s["started"], 1)
                pool.memset(three_halves[:, :], 1.5).then_inc(s["started"], 1)
                pool.wait_ge(s["started"], 2)

                def second_copies(t, v):
                    wait_apart(pool, idle_pool, 1, s["khi"], t + 1)
                    pool.tensor_copy(stack[v][:, :, 0, :, HD:2 * HD], stack[v][:, :, 0, :, 0:HD]).then_inc(s["kdup"], 1)
                    pool.tensor_copy(stack[v][:, :, 1, :, 2 * HD:3 * HD], stack[v][:, :, 1, :, 0:HD]).then_inc(s["kdup"], 1)

                def rsqrt(t):
                    STEPS = 12
                    pool.wait_ge(s["ss"], t + 1)
                    n = 0
                    for _ in range(3):
                        for out_, in0, in1, op_ in ((t0, y0, y0, ALU.mult), (t1, t0, vh, ALU.mult),
                                                    (t0, t1, three_halves, ALU.add), (y0, y0, t0, ALU.mult)):
                            if n:
                                pool.wait_ge(s["nw"], STEPS * t + n)
                            pool.tensor_tensor(out_[:, :], in0[:, :], in1[:, :], op_).then_inc(s["nw"], 1)
                            n += 1
                    pool.wait_ge(s["nw"], STEPS * t + n)

                def emit(i, u):
                    if normed and within(i - 2, T):
                        second_copies(i - 2, u % 2)
                    t = i - 8
                    if within(t, T):
                        factors(pool, res, s, t)
                    t = i - 5
                    if within(t, T):
                        v = (u - 1) % 2
                        wait(pool, s["oT"], t - 1)
                        wait_apart(pool, idle_pool, 2, s["o"], t + 1)
                        pool.tensor_copy(o_dup[v][:, :].rearrange("p (a r) -> p a r", a=4),
                                         o[v][:, :, :].rearrange("p h d -> p (h d)")[:, 2 * P:C].unsqueeze(1).broadcast_to([P, 4, REST]))\
                            .then_inc(s["odup"], 1)
                    t = i
                    if within(t, T):
                        pool.wait_ge(s["xhi"], 2 * t + 2)
                        pool.tensor_tensor(x_lo[:, :, :], xs[:, 0:2, :], x_hi[:, :, :], ALU.subtract).then_inc(s["xlo"], 1)
                        pool.wait_ge(s["xlo"], 2 * t + 1)
                        pool.tensor_tensor(x_rest[REST:2 * REST, :], xs[REST:2 * REST, 2, :], x_rest[REST:2 * REST, :],
                                           ALU.subtract).then_inc(s["xlo"], 1)
                        pool.wait_ge(s["xlo"], 2 * t + 2)
                    t = i - 1
                    if normed and within(t, T):
                        rsqrt(t)
                        pool.wait_ge(s["gk"], t + 1)
                        for n in range(2):
                            last = pool.tensor_tensor(qk[:, n, 1], qk[:, n, 1],
                                                      y0[:, 16 * n + 8:16 * n + 16].unsqueeze(2).broadcast_to([P, 8, HD]), ALU.mult)
                        last.then_inc(s["kn"], 1)
                    t = i - 6
                    if within(t, T):
                        pool.wait_ge(s["upd"], t + 1)
                        pool.tensor_tensor(res["x"][:, ds(t, 1), :], res["x"][:, ds(t, 1), :], upd[:, u % 2:u % 2 + 1, :], ALU.add)\
                            .then_inc(s["x"], 1)
                    if not normed and within(i - 1, T):
                        second_copies(i - 1, (u - 1) % 2)
                steps(pool, emit, FIRST, LAST, T - LAST + EXTRA, TURN)
                pool.wait_ge(s["rs"], 2 * T)

            @block.vector
            def _(dve):
                dve.memset(idle_dve[:, :], 0.0).then_inc(s["zero"], 1)
                for v in vals:
                    dve.memset(v[:, :, :, :], 0.0).then_inc(s["zero"], 1)
                dve.wait_ge(s["zero"], 1 + TURN)
                for v in vals:
                    for b in range(SEQS):
                        dve.memset(v[b * L:(b + 1) * L, b, :, HD:VW], 1.0).then_inc(s["init"], 1)

                def softmax_part(t, n):
                    dve.wait_ge(s["score"], 2 * t + n + 1)
                    dve.tensor_reduce(mx[:, 8 * n:8 * n + 8], sp_[:, n, :].rearrange("p (h q) -> p h q", h=8),
                                      AX.X, ALU.max).then_inc(s["mx"], 1)
                    dve.wait_ge(s["mx"], 2 * t + n + 1)
                    wait(dve, s["exp"], 2 * t + n - 1)
                    dve.tensor_tensor(sd[:, 8 * n:8 * n + 8, :], sp_[:, n, :].rearrange("p (h q) -> p h q", h=8),
                                      mx[:, 8 * n:8 * n + 8].unsqueeze(2).broadcast_to([P, 8, L]),
                                      ALU.subtract).then_inc(s["sub"], 1)

                def lo_part(t, v, j):
                    dve.wait_ge(s["khi"], t + 1)
                    dve.wait_ge(s["vals"], t + 1)
                    slot = 2 - j
                    src = qk[:, :, j] if normed else \
                        qp[:, :, j * HALF:(j + 1) * HALF].rearrange("p n (h d) -> p n h d", d=HD)
                    dve.tensor_tensor(stack[v][:, :, j, :, slot * HD:(slot + 1) * HD], src, stack[v][:, :, j, :, 0:HD],
                                      ALU.subtract).then_inc(s["klo"], 1)

                def emit(i, u):
                    if within(i - 3, T):
                        softmax_part(i - 3, 0)
                    if normed and within(i - 2, T):
                        lo_part(i - 2, u % 2, 0)
                    t = i
                    if within(t, T):
                        dve.wait_ge(s["xT"], t + 1)
                        wait(dve, s["xlo"], 2 * t)
                        b = scale[:, :, ds(SEQS * t, SEQS)].unsqueeze(3).broadcast_to([P, 3, SEQS, L])
                        dve.tensor_tensor(xs[:, :, :].rearrange("p c (b q) -> p c b q", b=SEQS),
                                          tp[:, XT_BANK, 0:3 * P].rearrange("p (c b q) -> p c b q", c=3, b=SEQS), b,
                                          ALU.mult).then_inc(s["xs"], 1)
                    if normed and within(i - 2, T):
                        lo_part(i - 2, u % 2, 1)
                    t = i - 2
                    if within(t, T):
                        dve.wait_ge(s["qTt"], 2 * t + 1)
                        wait(dve, s["score"], 2 * t)
                        q_second(t, 0)
                        dve.wait_ge(s["qTt"], 2 * t + 2)
                        q_second(t, 1)
                    t = i - 1
                    if normed and within(t, T):
                        dve.wait_ge(s["sq"], t + 1)
                        dve.tensor_reduce(ss[:, :].rearrange("p (n h) -> p n h", n=2),
                                          sq[:, :, :].rearrange("p n (h d) -> p n h d", d=HD), AX.X, ALU.add)\
                            .then_inc(s["rr"], 1)
                    t = i - 6
                    if within(t, T):
                        dve.wait_ge(s["proj"], t + 1)
                        dve.wait_ge(gate_in[u % 2], parity_count(t, u % 2, 32))
                        wait(dve, s["x"], t - 1)
                        dve.tensor_tensor(upd[:, u % 2, :], op[:, 0, 0:C], gate[u % 2][:, :], ALU.mult).then_inc(s["upd"], 1)
                    t = i - 1
                    if normed and within(t, T):
                        dve.wait_ge(s["rr"], t + 1)
                        dve.tensor_scalar(vh[:, :], ss[:, :], -0.5 / HD, -0.5 * EPS, ALU.mult, ALU.add).then_inc(s["vh"], 1)
                        dve.wait_ge(s["vh"], t + 1)
                        wait(dve, s["kn"], t)
                        dve.tensor_scalar(y0[:, :].bitcast(I32), vh[:, :].bitcast(I32), -0.5, GUESS, ALU.mult, ALU.add).then_inc(s["ss"], 1)
                    t = i - 1
                    if normed and within(t, T):
                        dve.wait_ge(s["vals"], t + 1)
                        wait(dve, s["klo"], 2 * t)
                        for n in range(2):
                            last = dve.tensor_tensor(qk[:, n, 1], qp[:, n, HALF:2 * HALF].rearrange("p (h d) -> p h d", d=HD),
                                                     gains[:, :].unsqueeze(1).broadcast_to([P, 8, HD]), ALU.mult)
                        last.then_inc(s["gk"], 1)
                    if within(i - 3, T):
                        softmax_part(i - 3, 1)
                    if not normed and within(i - 1, T):
                        lo_part(i - 1, (u - 1) % 2, 0)
                        lo_part(i - 1, (u - 1) % 2, 1)
                    t = i - 4
                    if within(t, T):
                        dve.wait_ge(s["pv"], t + 1)
                        dve.reciprocal(rc[:, :, :], op[:, :, 0:16 * VW].rearrange("p n (g v) -> p n g v", v=VW)[:, :, :, HD])\
                            .then_inc(s["rc"], 1)
                        dve.wait_ge(s["rc"], t + 1)
                        wait(dve, s["oT"], t - 1)
                        for j in range(2):
                            for b in range(SEQS):
                                rows, dst = slice(j * L, (j + 1) * L), slice(b * L, (b + 1) * L)
                                src = op[rows, :, 0:16 * VW].rearrange("p n (g a v) -> p n g a v", g=4, v=VW)[:, :, :, 2 * b + j, 0:HD]
                                fac = rc[rows, :, :].rearrange("p n (g a) -> p n g a", g=4)[:, :, :, 2 * b + j]
                                last = dve.tensor_tensor(
                                    o[u % 2][dst, :, :].rearrange("p (n g j) d -> p n g j d", n=2, j=2)[:, :, :, j, :], src,
                                    fac.unsqueeze(3).broadcast_to([L, 2, 4, HD]), ALU.mult)
                        last.then_inc(s["o"], 1)
                    t = i - 5
                    if within(t, T):
                        dve.wait_ge(s["ohi"], 2 * t + 2)
                        dve.tensor_tensor(o_lo[:, :, :], tp[:, OT_BANK, 0:2 * P].rearrange("p (c q) -> p c q", c=2), o_hi[:, :, :],
                                          ALU.subtract)
                        dve.tensor_tensor(o_rest[REST:2 * REST, :], tp[REST:2 * REST, OT_BANK, 2 * P:3 * P],
                                          o_rest[REST:2 * REST, :], ALU.subtract).then_inc(s["olo"], 1)
                    t = i - 7
                    if within(t, T):
                        statistics(dve, res, s, bn, mv, idle_dve, 3, t)
                    t = i - 1
                    if normed and within(t, T):
                        dve.wait_ge(s["nw"], 12 * t + 12)
                        dve.wait_ge(s["qraw"], t + 1)
                        for n in range(2):
                            last = dve.tensor_tensor(qk[:, n, 0], qk[:, n, 0],
                                                     y0[:, 16 * n:16 * n + 8].unsqueeze(2).broadcast_to([P, 8, HD]), ALU.mult)
                        last.then_inc(s["qn"], 1)

                def q_second(t, n):
                    dve.tensor_copy(qT[L:P, 4 * n:4 * n + 4, :, 1, :],
                                    tp[L:P, QT_BANK[n], :].rearrange("p (g b q) -> p g b q", g=4, b=SEQS)).then_inc(s["qTd"], 1)
                steps(dve, emit, FIRST, LAST, T - LAST + EXTRA, TURN)

            @block.scalar
            def _(act):
                act.activation(x_rest[BIAS:BIAS + 2 * SEQS, :], res["hot"][BIAS:BIAS + 2 * SEQS, 0:P], ACT.Copy)
                act.activation(o_rest[BIAS:BIAS + 2, :], res["hot"][BIAS:BIAS + 2, ONES:], ACT.Copy).then_inc(s["init"], 1)
                act.wait_ge(s["init"], 4 + SEQS * TURN)
                normalise(act, xn, res, 0).then_inc(s["xn"], 1)

                def exp(t, n):
                    act.wait_ge(s["sub"], 2 * t + n + 1)
                    wait(act, s["prT"], 2 * t + n - 1)
                    act.activation(pr[:, 8 * n:8 * n + 8, :], sd[:, 8 * n:8 * n + 8, :], ACT.Exp).then_inc(s["exp"], 1)

                def hi_parts(t, v, src):
                    wait(act, s["kTt"], 2 * (t - 1))
                    act.activation(stack[v][:, :, :, :, 0:HD].rearrange("p n s h d -> p n (s h) d"), src, ACT.Copy).then_inc(s["khi"], 1)

                def values(t, v):
                    wait(act, s["pv"], t - TURN + 1)
                    for b in range(SEQS):
                        rows = slice(b * L, (b + 1) * L)
                        last = act.activation(vals[v][rows, b, :, 0:HD].rearrange("p (n h) d -> p n h d", n=2),
                                              qp[rows, :, 2 * HALF:QKVH].rearrange("p n (h d) -> p n h d", d=HD), ACT.Copy)
                    last.then_inc(s["vals"], 1)

                def emit(i, u):
                    t = i - 1
                    if normed and within(t, T):
                        act.wait_ge(s["qkv"], t + 1)
                        wait(act, s["rr"], t)
                        act.activation(sq[:, :, :], qp[:, :, 0:2 * HALF], ACT.Square).then_inc(s["sq"], 1)
                    if within(i - 3, T):
                        exp(i - 3, 0)
                    t = i - 2
                    if within(t, T):
                        for n in range(2):
                            act.wait_ge(s["qTt"], 2 * t + n + 1)
                            if n == 0:
                                wait(act, s["score"], 2 * t)
                            act.activation(qT[0:L, 4 * n:4 * n + 4, :, 0, :],
                                           tp[0:L, QT_BANK[n], :].rearrange("p (g b q) -> p g b q", g=4, b=SEQS), ACT.Copy).then_inc(s["qTa"], 1)
                    t = i
                    if within(t, T):
                        act.wait_ge(s["xs"], t + 1)
                        wait(act, s["qkv"], t)
                        act.activation(x_hi[:, :, :], xs[:, 0:2, :], ACT.Copy).then_inc(s["xhi"], 1)
                        act.activation(x_rest[0:BIAS, :], xs[0:BIAS, 2, :], ACT.Copy).then_inc(s["xhi"], 1)
                    t = i - 1
                    if within(t, T):
                        act.wait_ge(s["qkv"], t + 1)
                        if normed:
                            wait(act, s["klo"], 2 * t)
                            act.activation(qk[:, :, 0].rearrange("p n h d -> p n (h d)"), qp[:, :, 0:HALF], ACT.Copy).then_inc(s["qraw"], 1)
                        else:
                            hi_parts(t, (u - 1) % 2, qp[:, :, 0:2 * HALF].rearrange("p n (h d) -> p n h d", d=HD))
                        values(t, (u - 1) % TURN)
                    t = i - 2
                    if within(t, T):
                        for n in range(2):
                            act.wait_ge(s["kTt"], 2 * t + n + 1)
                            act.activation(kT[:, 4 * n:4 * n + 4, :, :],
                                           tp[:, KT_BANK[n], :].rearrange("p (g b q) -> p g b q", g=4, b=SEQS), ACT.Copy).then_inc(s["kTa"], 1)
                    if within(i - 3, T):
                        exp(i - 3, 1)
                    t = i - 5
                    if within(t, T):
                        act.wait_ge(s["oT"], t + 1)
                        wait(act, s["proj"], t)
                        act.activation(o_hi[:, :, :], tp[:, OT_BANK, 0:2 * P].rearrange("p (c q) -> p c q", c=2), ACT.Copy).then_inc(s["ohi"], 1)
                        act.activation(o_rest[0:BIAS, :], tp[0:BIAS, OT_BANK, 2 * P:3 * P], ACT.Copy).then_inc(s["ohi"], 1)
                    t = i + 1
                    if within(t, T):
                        act.wait_ge(s["xT"], t)
                        normalise(act, xn, res, t).then_inc(s["xn"], 1)
                    t = i - 3
                    if within(t, T):
                        for n in range(2):
                            act.wait_ge(s["prT"], 2 * t + n + 1)
                            wait(act, s["pv"], t)
                            act.activation(prT[:, 4 * n:4 * n + 4, :], tp[:, PT_BANK[n], :].rearrange("p (g q) -> p g q", g=4),
                                           ACT.Copy).then_inc(s["prTe"], 1)
                    t = i - 1
                    if normed and within(t, T):
                        act.wait_ge(s["qn"], t + 1)
                        act.wait_ge(s["kn"], t + 1)
                        hi_parts(t, (u - 1) % 2, qk[:, :, :, :, :].rearrange("p n s h d -> p n (s h) d"))
                steps(act, emit, FIRST, LAST, T - LAST + EXTRA, TURN)

            @block.tensor
            def _(pe):
                ident, ident_r = res["ident"], res["ident_r"]

                def qkv(t, v, n):
                    if n == 0:
                        pe.wait_ge(s["xhi"], 2 * t + 2)
                        pe.wait_ge(s["xlo"], 2 * t + 2)
                        pe.wait_ge(rows_in[v], parity_count(t, v, 32))
                        if normed:
                            wait(pe, s["gk"], t)
                        else:
                            wait(pe, s["klo"], 2 * t)
                        wait(pe, s["vals"], t)
                    return three(pe, qp[:, n, 0:QKVH], slice(n * QKVH, (n + 1) * QKVH), (x_hi, x_lo, x_rest),
                                 (wqkv_hi, wqkv_lo, wqkv_rest[v]), BIAS + 2 * SEQS)

                def stack_transposes(t, v, j, n):
                    pe.wait_ge(s["klo"], 2 * t + j + 1)
                    pe.wait_ge(s["kdup"], 2 * t + j + 1)
                    bank = (QT_BANK, KT_BANK)[j][n]
                    for g in range(4):
                        last = pe.transpose(tp[:, bank, g * P:(g + 1) * P].bitcast(F32R),
                                            stack[v][:, n, j, 2 * g:2 * g + 2, :].rearrange("p h r -> p (h r)"), ident_r[:, :])
                    last.then_inc(s["qTt" if j == 0 else "kTt"], 1)

                def emit(i, u):
                    if within(i - 1, T):
                        qkv(i - 1, (u - 1) % 2, 0)
                    t = i
                    if within(t, T):
                        pe.wait_ge(s["xn"], t + 1)
                        wait(pe, s["prTe"], 2 * (i - 4) + 1)
                        if isinstance(t, int):
                            wait(pe, s["xs"], t)
                        transposes(pe, tp[:, XT_BANK], xn, xn[:, 2 * P:3 * P], ident).then_inc(s["xT"], 1)
                    if within(i - 1, T):
                        qkv(i - 1, (u - 1) % 2, 1).then_inc(s["qkv"], 1)
                    t = i - 2
                    if within(t, T):
                        wait(pe, s["prTe"], 2 * (i - 4) + 2)
                        stack_transposes(t, u % 2, 0, 0)
                        pe.wait_ge(s["xs"], upto(i))
                        stack_transposes(t, u % 2, 0, 1)
                    t = i - 6
                    if within(t, T):
                        pe.wait_ge(s["ohi"], 2 * t + 2)
                        pe.wait_ge(s["olo"], t + 1)
                        pe.wait_ge(s["o"], upto(t + 1))
                        if isinstance(t, int):
                            wait(pe, s["upd"], t)
                        three(pe, op[:, 0, 0:C], slice(0, C), (o_hi, o_lo, o_rest), (wo_hi, wo_lo, wo_rest), BIAS + 2)\
                            .then_inc(s["proj"], 1)
                    t = i - 2
                    if within(t, T):
                        for n in range(2):
                            pe.wait_ge(s["qTa"], 2 * t + n + 1)
                            pe.wait_ge(s["qTd"], 2 * t + n + 1)
                            stack_transposes(t, u % 2, 1, n)
                    t = i - 4
                    if within(t, T):
                        pe.wait_ge(s["prTe"], 2 * t + 2)
                        wait(pe, s["o"], t)
                        for p in (4, 5, 6, 7, 0, 1, 2, 3):
                            if p == 0:
                                wait(pe, s["upd"], t - 1)
                            last = pe.matmul(op[:, p // 4, (p % 4) * 4 * VW:(p % 4 + 1) * 4 * VW], prT[:, p, :],
                                             vals[u % TURN][:, :, 2 * p:2 * p + 2, :].rearrange("p b j v -> p b (j v)"),
                                             start=True, stop=True)
                        last.then_inc(s["pv"], 1)
                    t = i - 5
                    if within(t, T):
                        v = (u - 1) % 2
                        pe.wait_ge(s["o"], t + 1)
                        pe.wait_ge(s["odup"], t + 1)
                        pe.wait_ge(s["kTa"], 2 * upto(t + 3) - 1)
                        transposes(pe, tp[:, OT_BANK], o[v][:, :, :].rearrange("p h d -> p (h d)"), o_dup[v][:, :], ident).then_inc(s["oT"], 1)
                    t = i - 2
                    if within(t, T):
                        for n in range(2):
                            pe.wait_ge(s["kTa"], 2 * t + n + 1)
                            wait(pe, s["sub"], 2 * t + n - 1)
                            for p in range(4 * n, 4 * n + 4):
                                for b in range(SEQS):
                                    c = (2 * p + b) % 8
                                    last = pe.matmul(sp_[:, n, c * L:(c + 1) * L],
                                                     qT[:, p, b, :, :].rearrange("p j q -> p (j q)"), kT[:, p, b, :], start=True, stop=True)
                            last.then_inc(s["score"], 1)
                    t = i - 3
                    if within(t, T):
                        for n in range(2):
                            pe.wait_ge(s["exp"], 2 * t + n + 1)
                            if n == 0:
                                pe.wait_ge(s["kTa"], 2 * upto(t + 1))
                            else:
                                wait(pe, s["ohi"], 2 * (t - 2) + 2)
                                wait(pe, s["olo"], t - 2 + 1)
                            for g in range(4):
                                p = 4 * n + g
                                last = pe.transpose(tp[:, PT_BANK[n], g * P:(g + 1) * P],
                                                    pr[:, 2 * p:2 * p + 2, :].rearrange("p b q -> p (b q)"), ident[:, :])
                            last.then_inc(s["prT"], 1)
                steps(pe, emit, FIRST, LAST, T - LAST + EXTRA, TURN)


def mlp(nc, w, res, dram, out, l):
    with ExitStack() as ctx:
        k = Kit(nc, ctx, f"mlp{l}_")
        w1 = k.sb("w1_hi", [P, 2, FF], F32R), k.sb("w1_lo", [P, 2, FF], F32R), [k.sb(f"w1_rest{u}", [P, FF], F32R) for u in range(2)]
        w2 = k.sb("w2_hi", [P, MT, C], F32R), k.sb("w2_lo", [P, MT, C], F32R)
        b2 = k.sb("b2", [2, C], F32R)
        mlp_weights(nc, w, res, dram, l, w1, w2, b2)
        mlp_groups(nc, res, dram, out, l, w1, w2, b2)


def mlp_weights(nc, w, res, dram, l, w1, w2, b2):
    w1_hi, w1_lo, w1_rest = w1
    w2_hi, w2_lo = w2
    BANKS, BN = 3, FF // 3
    with ExitStack() as ctx:
        k = Kit(nc, ctx, f"mw{l}_")
        raw = k.sb("raw", [P, 3, FF])
        raw2 = k.sb("raw2", [P, MT, C])
        braw, braw_hi = k.sb("braw", [2, C]), k.sb("braw_hi", [2, C], F32R)
        rows_hi, rows_lo = k.sb("rows_hi", [P, BANKS, BN], F32R), k.sb("rows_lo", [P, BANKS, BN], F32R)
        rps = k.ps("rps", [P, BANKS, 512])
        w_in, w2_in = k.sem("w_in"), k.sem("w2_in")
        hi_done, hi2_done, rows_done, rhi_done, rlo_done, rows_out = (
            k.sem(n) for n in ("hi", "hi2", "rows", "rhi", "rlo", "rows_out"))
        shift = res[f"adapt{l}{SHIFT_MLP}"]
        with nc.Block() as block:

            @block.sync
            def _(sp):
                w1d, w2d = w[f"fc1_w{l}"], w[f"fc2_w{l}"]
                for c in range(2):
                    sp.dma_start(raw[:, c, :], w1d[c * P:(c + 1) * P, :]).then_inc(w_in, 16)
                sp.dma_start(raw[0:REST, 2, :], w1d[2 * P:C, :]).then_inc(w_in, 16)
                sp.dma_start(raw[REST:REST + 1, 2, :], w[f"fc1_b{l}"]).then_inc(w_in, 16)
                sp.dma_start(raw2[:, :, :], w2d.rearrange("(m p) n -> p m n", p=P)).then_inc(w2_in, 16)
                sp.dma_start(braw[:, :], w[f"fc2_b{l}"].broadcast_to([2, C])).then_inc(w2_in, 16)
                for n, (done, rows) in enumerate(((rhi_done, rows_hi), (rlo_done, rows_lo))):
                    sp.wait_ge(done, 1)
                    sp.dma_start(dram[f"fc_rows{l}"][n], rows[:, :, :].rearrange("p a b -> p (a b)").bitcast(F32)).then_inc(rows_out, 16)
                sp.wait_ge(rows_out, 32)

            @block.scalar
            def _(act):
                act.wait_ge(w_in, 64)
                act.activation(w1_hi[:, :, :], raw[:, 0:2, :], ACT.Copy).then_inc(hi_done, 1)
                for u in range(2):
                    act.activation(w1_rest[u][0:REST, :], raw[0:REST, 2, :], ACT.Copy)
                    act.activation(w1_rest[u][REST:2 * REST, :], raw[0:REST, 2, :], ACT.Copy).then_inc(hi_done, 1)
                act.wait_ge(w2_in, 32)
                act.activation(w2_hi[:, :, :], raw2[:, :, :], ACT.Copy).then_inc(hi2_done, 1)
                act.activation(braw_hi[:, :], braw[:, :], ACT.Copy).then_inc(hi2_done, 1)
                act.wait_ge(rows_done, 1)
                act.activation(rows_hi[:, :, :], rps[:, :, 0:BN], ACT.Copy).then_inc(rhi_done, 1)

            @block.vector
            def _(dve):
                dve.wait_ge(hi_done, 3)
                dve.tensor_tensor(w1_lo[:, :, :], raw[:, 0:2, :], w1_hi[:, :, :], ALU.subtract)
                for u in range(2):
                    dve.tensor_tensor(w1_rest[u][2 * REST:3 * REST, :], raw[0:REST, 2, :], w1_rest[u][0:REST, :], ALU.subtract)
                dve.wait_ge(hi2_done, 2)
                dve.tensor_tensor(w2_lo[:, :, :], raw2[:, :, :], w2_hi[:, :, :], ALU.subtract)
                dve.scalar_tensor_tensor(b2[:, :], braw_hi[:, :], res["hot"][0:2, PICK:PICK + 1], braw[:, :], ALU.mult, ALU.add)
                dve.wait_ge(rhi_done, 1)
                dve.tensor_tensor(rows_lo[:, :, :], rps[:, :, 0:BN], rows_hi[:, :, :], ALU.subtract).then_inc(rlo_done, 1)

            @block.tensor
            def _(pe):
                pe.wait_ge(w_in, 64)
                for n in range(BANKS):
                    for c in range(3):
                        kk = P if c < 2 else REST + 1
                        mm = pe.matmul(rps[:, n, 0:BN], shift[0:kk, c, :], raw[0:kk, c, n * BN:(n + 1) * BN],
                                       start=(c == 0), stop=(c == 2))
                mm.then_inc(rows_done, 1)


def mlp_groups(nc, res, dram, out, l, w1, w2, b2):
    w1_hi, w1_lo, w1_rest = w1
    w2_hi, w2_lo = w2
    NG = T // GROUP
    LAG = 2
    with ExitStack() as ctx:
        k = Kit(nc, ctx, f"mg{l}_")
        xn = k.sb("xn", [P, 3 * P])
        xs = k.sb("xs", [P, 3, P])
        x_hi = [k.sb(f"x_hi{u}", [P, 2, GT], F32R) for u in range(2)]
        x_lo = [k.sb(f"x_lo{u}", [P, 2, GT], F32R) for u in range(2)]
        x_rest = [k.sb(f"x_rest{u}", [P, GT], F32R) for u in range(2)]
        hid = k.sb("hid", [P, 3, GT])
        h_hi, h_lo = k.sb("h_hi", [P, 3, GT], F32R), k.sb("h_lo", [P, 3, GT], F32R)
        ones = k.sb("ones", [2, P], F32R)
        gate = [k.sb(f"gate{u}", [P, GROUP, C]) for u in range(2)]
        upd = k.sb("upd", [P, 2, C])
        bn, mv = k.sb("bn", [P, 6]), k.sb("mv", [P, 2])
        idle_dve = k.sb("idle_dve", [P, 8])
        tp = k.ps("tp", [P, 512])
        hp = [k.ps(f"hp{i}", [P, GT]) for i in range(3)]
        yp = k.ps("yp", [P, GROUP, 512])
        s = {n: k.sem(n) for n in ("started", "init", "xn", "xT", "xs", "xhi", "xlo", "fc1", "gelu", "hhi", "hlo", "fc2", "upd", "x", "bn", "ve", "rs", "out")}
        rows_in = [k.sem(f"rows_in{u}") for u in range(2)]
        gate_in = [k.sem(f"gate_in{u}") for u in range(2)]
        scale = res[f"adapt{l}{SCALE_MLP}"]
        FIRST, EXTRA = 4, 3
        PREP = (1, 3, 5, 7)

        with nc.Block() as block:

            @block.sync
            def _(sp):
                def emit(i, u):
                    if within(i, NG):
                        wait(sp, s["fc1"], MT * (i - 1))
                        for n in range(2):
                            r = BIAS + GS * n
                            sp.dma_start(w1_rest[u][r:r + GS, :].bitcast(F32), dram[f"fc_rows{l}"][n, ds(GS * i, GS), :]).then_inc(rows_in[u], 16)
                        wait(sp, s["upd"], GROUP * (i - 1))
                        for b in range(SEQS):
                            src = dram[f"gate{l}1"][ds(GS * i, GS), :].rearrange("(j b) c -> b j c", b=SEQS)[b:b + 1]
                            sp.dma_start(gate[u][b * L:(b + 1) * L, :, :], src.broadcast_to([L, GROUP, C])).then_inc(gate_in[u], 16)
                    if l == 1 and within(i - 2, NG):
                        sp.wait_ge(s["x"], GROUP * (i - 1))
                        sp.dma_start(out[ds(GROUP * (i - 2), GROUP)].rearrange("t p c -> p t c"),
                                     res["x"][:, ds(GROUP * (i - 2), GROUP), :]).then_inc(s["out"], 16)
                steps(sp, emit, FIRST, NG, EXTRA)
                if l == 1:
                    sp.wait_ge(s["out"], 16 * NG)

            @block.gpsimd
            def _(pool):
                def prepare(i, u, j):
                    n = GROUP * i + j
                    pool.wait_ge(s["xhi"], 2 * n + 2)
                    cols = slice(j * P, (j + 1) * P)
                    pool.tensor_tensor(x_lo[u][:, :, cols], xs[:, 0:2, :], x_hi[u][:, :, cols], ALU.subtract).then_inc(s["xlo"], 1)
                    pool.wait_ge(s["xlo"], 2 * n + 1)
                    pool.tensor_tensor(x_rest[u][REST:2 * REST, cols], xs[REST:2 * REST, 2, :], x_rest[u][REST:2 * REST, cols],
                                       ALU.subtract).then_inc(s["xlo"], 1)
                    pool.wait_ge(s["xlo"], 2 * n + 2)

                def emit(i, u):
                    g = i - 2
                    if within(g, NG):
                        for j in range(GROUP):
                            n = GROUP * g + j
                            pool.wait_ge(s["upd"], n + 1)
                            pool.tensor_tensor(res["x"][:, ds(n, 1), :], res["x"][:, ds(n, 1), :], upd[:, j % 2:j % 2 + 1, :],
                                               ALU.add).then_inc(s["x"], 1)
                    for j in range(GROUP):
                        if within(i, NG):
                            prepare(i, u, j)
                        if l == 0 and within(g, NG):
                            n = GROUP * g + j
                            factors(pool, res, s, n)
                steps(pool, emit, FIRST, NG, EXTRA)

            @block.vector
            def _(dve):
                dve.memset(idle_dve[:, :], 0.0).then_inc(s["started"], 1)
                dve.wait_ge(s["started"], 1)

                def prepare(i, u, j):
                    n = GROUP * i + j
                    dve.wait_ge(s["xT"], n + 1)
                    wait(dve, s["xlo"], 2 * n)
                    b = scale[:, :, ds(SEQS * n, SEQS)].unsqueeze(3).broadcast_to([P, 3, SEQS, L])
                    dve.tensor_tensor(xs[:, :, :].rearrange("p c (b q) -> p c b q", b=SEQS),
                                      tp[:, 0:3 * P].rearrange("p (c b q) -> p c b q", c=3, b=SEQS), b, ALU.mult).then_inc(s["xs"], 1)

                def emit(i, u):
                    g = i - 2
                    if within(g, NG):
                        dve.wait_ge(gate_in[u], parity_count(g, u, 32))
                        dve.wait_ge(s["fc2"], MT * (g + 1))
                        for j in range(GROUP):
                            n = GROUP * g + j
                            wait(dve, s["x"], n - 1)
                            dve.tensor_tensor(upd[:, j % 2, :], yp[:, j, 0:C], gate[u][:, j, :], ALU.mult).then_inc(s["upd"], 1)
                    g = i - 1
                    for m in range(MT):
                        if within(g, NG):
                            dve.wait_ge(s["gelu"], MT * g + m + 1)
                            wait(dve, s["fc2"], MT * g + m - 2)
                            dve.tensor_copy(h_hi[:, m % 3, :], hid[:, m % 3, :]).then_inc(s["hhi"], 1)
                            dve.wait_ge(s["hhi"], MT * g + m + 1)
                            dve.tensor_tensor(h_lo[:, m % 3, :], hid[:, m % 3, :], h_hi[:, m % 3, :], ALU.subtract).then_inc(s["hlo"], 1)
                        if within(i, NG) and m in PREP:
                            prepare(i, u, PREP.index(m))
                        if l == 0 and within(i - 2, NG) and m in PREP:
                            n = GROUP * (i - 2) + PREP.index(m)
                            statistics(dve, res, s, bn, mv, idle_dve, 4, n)
                steps(dve, emit, FIRST, NG, EXTRA)

            @block.scalar
            def _(act):
                for u in range(2):
                    act.activation(x_rest[u][BIAS:BIAS + 2 * GS, :], res["hot"][BIAS:BIAS + 2 * GS, P:P + GT], ACT.Copy)
                act.activation(ones[:, :], res["hot"][0:2, ONES:], ACT.Copy).then_inc(s["init"], 1)

                def prepare(i, u, j):
                    n = GROUP * i + j
                    cols = slice(j * P, (j + 1) * P)
                    wait(act, s["xT"], n)
                    normalise(act, xn, res, n).then_inc(s["xn"], 1)
                    act.wait_ge(s["xs"], n + 1)
                    if j == 0:
                        wait(act, s["fc1"], MT * (i - 1))
                    act.activation(x_hi[u][:, :, cols], xs[:, 0:2, :], ACT.Copy).then_inc(s["xhi"], 1)
                    act.activation(x_rest[u][0:BIAS, cols], xs[0:BIAS, 2, :], ACT.Copy).then_inc(s["xhi"], 1)

                def emit(i, u):
                    g = i - 1
                    for m in range(MT):
                        if within(g, NG):
                            act.wait_ge(s["fc1"], MT * g + m + 1)
                            wait(act, s["hlo"], MT * g + m - 2)
                            act.activation(hid[:, m % 3, :], hp[m % 3][:, :], ACT.Gelu_apprx_tanh).then_inc(s["gelu"], 1)
                        if within(i, NG) and m in PREP:
                            prepare(i, u, PREP.index(m))
                steps(act, emit, FIRST, NG, EXTRA)

            @block.tensor
            def _(pe):
                pe.wait_ge(s["init"], 1)

                def fc1(g, u, m):
                    wait(pe, s["gelu"], MT * g + m - 2)
                    cols = slice(m * P, (m + 1) * P)
                    dst, rest = hp[m % 3][:, :], BIAS + 2 * GS
                    pe.matmul(dst, w1_rest[u][0:rest, cols], x_rest[u][0:rest, :], start=True, stop=False)
                    for c in range(2):
                        pe.matmul(dst, w1_hi[:, c, cols], x_hi[u][:, c, :], start=False, stop=False)
                        pe.matmul(dst, w1_hi[:, c, cols], x_lo[u][:, c, :], start=False, stop=False)
                        last = pe.matmul(dst, w1_lo[:, c, cols], x_hi[u][:, c, :], start=False, stop=(c == 1))
                    last.then_inc(s["fc1"], 1)

                def fc2(g, m):
                    pe.wait_ge(s["hlo"], MT * g + m + 1)
                    if m == 0:
                        wait(pe, s["upd"], GROUP * g)
                    for j in range(GROUP):
                        cols, dst, r = slice(j * P, (j + 1) * P), yp[:, j, 0:C], m % 3
                        if m == 0:
                            pe.matmul(dst, ones[:, :], b2[:, :], start=True, stop=False)
                        pe.matmul(dst, h_hi[:, r, cols], w2_hi[:, m, :], start=False, stop=False)
                        pe.matmul(dst, h_hi[:, r, cols], w2_lo[:, m, :], start=False, stop=False)
                        last = pe.matmul(dst, h_lo[:, r, cols], w2_hi[:, m, :], start=False, stop=(m == MT - 1))
                    last.then_inc(s["fc2"], 1)

                def emit(i, u):
                    g = i - 1
                    if within(g, NG):
                        pe.wait_ge(s["xhi"], 2 * GROUP * (g + 1))
                        pe.wait_ge(s["xlo"], 2 * GROUP * (g + 1))
                        pe.wait_ge(rows_in[1 - u], parity_count(g, 1 - u, 32))
                    for m in range(MT + LAG):
                        if within(g, NG):
                            if m < MT:
                                fc1(g, 1 - u, m)
                            if m >= LAG:
                                fc2(g, m - LAG)
                        if within(i, NG) and m in PREP:
                            n = GROUP * i + PREP.index(m)
                            pe.wait_ge(s["xn"], n + 1)
                            wait(pe, s["xs"], n)
                            transposes(pe, tp, xn, xn[:, 2 * P:3 * P], res["ident"]).then_inc(s["xT"], 1)
                steps(pe, emit, FIRST, NG, EXTRA)


def program(nc, w, out):
    with ExitStack() as ctx:
        k = Kit(nc, ctx, "")
        res = {
            "x": k.sb("x", [P, T, C]),
            "ident": k.sb("ident", [P, P]), "ident_r": k.sb("ident_r", [P, P], F32R),
            "hot": k.sb("hot", [P, ONES + P]),
            "nm": k.sb("nm", [P, T]), "nb": k.sb("nb", [P, T]), "ve": k.sb("ve", [P, T]), "rs": k.sb("rs", [P, T]), "mhalf": k.sb("mhalf", [P, T]),
        }
        dram = {}
        for l in range(2):
            for part in (SHIFT_MSA, SCALE_MSA, SHIFT_MLP, SCALE_MLP):
                res[f"adapt{l}{part}"] = k.sb(f"adapt{l}{part}", [P, 3, P])
            dram[f"qkv_rows{l}"] = nc.dram_tensor(f"qkv_rows{l}", (2, B, 2 * QKVH), F32, kind="Internal").ap()
            dram[f"fc_rows{l}"] = nc.dram_tensor(f"fc_rows{l}", (2, B, FF), F32, kind="Internal").ap()
            for g in range(2):
                dram[f"gate{l}{g}"] = nc.dram_tensor(f"gate{l}{g}", (B, C), F32, kind="Internal").ap()
        modulation(nc, w, res, dram)
        for l in range(2):
            attention(nc, w, res, dram, l)
            mlp(nc, w, res, dram, out, l)


def constants():
    import numpy as np
    hot = np.zeros((2 * GS, ONES + P), np.float32)
    for r in range(2 * GS):
        if r < 2 * SEQS:
            hot[r, 0:P] = np.arange(P) // L == r % SEQS
        hot[r, P:P + GT] = np.arange(GT) // L == r % GS
    hot[1, PICK] = -1.0
    hot[:, ONES:] = 1.0
    return hot, np.eye(P, dtype=np.float32)


NAMES = {"x": "x", "cond_1152": "cond_1152", "gain0": "L0_cond_g_q", "gain1": "L0_cond_g_k"}
for _l, _names in enumerate((
        dict(mod="w_mod b_mod", qkv="w_qkv b_qkv", o="w_proj b_proj", fc1="w1 b1", fc2="w2 b2"),
        dict(mod="W_ada b_ada", qkv="W_qkv b_qkv", o="W_proj b_proj", fc1="W_fc1 b_fc1", fc2="W_fc2 b_fc2"))):
    for _k, _v in _names.items():
        for _kind, _n in zip("wb", _v.split()):
            NAMES[f"{_k}_{_kind}{_l}"] = f"L{_l}_cond_{_n}"


def kernel(**inputs):
    import numpy as np
    import concourse.bacc as bacc
    from concourse.bass_utils import run_bass_kernel_spmd

    nc = bacc.Bacc("TRN2", target_bir_lowering=False, num_devices=1)
    hot, ident = constants()
    arrays = {"hot": hot, "ident": ident}
    for name, theirs in NAMES.items():
        a = np.ascontiguousarray(inputs[theirs])
        if name == "x":
            a = a.reshape(T, P, C)
        if a.ndim == 1:
            a = a.reshape(1, -1)
        arrays[name] = a
    w = {n: nc.dram_tensor(f"in_{n}", a.shape, mybir.dt.from_np(a.dtype), kind="ExternalInput").ap() for n, a in arrays.items()}
    out = nc.dram_tensor("out_x", (T, P, C), F32, kind="ExternalOutput").ap()
    program(nc, w, out)
    r = run_bass_kernel_spmd(nc, [{f"in_{n}": a for n, a in arrays.items()}], core_ids=[0])
    return r.results[0]["out_x"].reshape(B, L, C)
```
